# Optimizing a Trainium2 kernel written in Bass

```python
import numpy as np
import jax
import jax.numpy as jnp

def _softmax(x, axis=-1):
    return jax.nn.softmax(x, axis=axis)

def _gelu(x):
    return jax.nn.gelu(x, approximate=True)

def _silu(x):
    return jax.nn.silu(x)

def _sigmoid(x):
    return jax.nn.sigmoid(x)

def _layernorm(x, axis=-1, eps=1e-05):
    m = jnp.mean(x, axis=axis, keepdims=True)
    v = jnp.var(x, axis=axis, keepdims=True)
    return (x - m) / jnp.sqrt(v + eps)

def _scatter_add(tgt, idx, src, axis=0):
    return tgt.at[idx].add(src)

def _segment_sum(src, seg, n):
    return jax.ops.segment_sum(src, seg, n)
kernel_name = 'mk_xattn_ffn_d1_seqx_r4_be12e7'

def setup_inputs(seed: int=0):
    np.random.seed(seed)
    _w = jnp.asarray

    def _rec_inputs():
        import jax
        import jax.numpy as jnp
        _rk = jax.random.key(seed)
        x = -0.0003929 + 0.9999 * jax.random.normal(jax.random.fold_in(_rk, 1), (128, 128, 256), jnp.float32)
        _lenS = 128 - jax.random.randint(jax.random.fold_in(_rk, 7), (128,), 0, max(1, 128 // 4) + 1, jnp.int32)
        _lenS2 = 128 - jax.random.randint(jax.random.fold_in(_rk, 8), (128,), 0, max(1, 128 // 4) + 1, jnp.int32)
        _ctx_768P = jax.random.normal(jax.random.fold_in(_rk, 11), (128, 16, 192), jnp.float32)
        _ctx_768c = jax.random.dirichlet(jax.random.fold_in(_rk, 511), 0.3 * jnp.ones((16,), jnp.float32), (128, 128))
        _ctx_768t = jnp.einsum('bsk,bkd->bsd', _ctx_768c, _ctx_768P)
        _ctx_768t = _ctx_768t * jax.lax.rsqrt(jnp.mean(jnp.square(_ctx_768t)) + 1e-12) * 0.953939
        ctx_768 = 0.00095986 + 0.999812 * (_ctx_768t + 0.3 * jax.random.normal(jax.random.fold_in(_rk, 611), (128, 128, 192), jnp.float32))
        _validS = jnp.arange(128)[None, :] < _lenS[:, None]
        _validS2 = jnp.arange(128)[None, :] < _lenS2[:, None]
        _causal = jnp.tril(jnp.ones((128, 128), dtype=bool))
        mask_BxS2_bf1 = jnp.ones((128, 128), dtype=bool)
        return (x, ctx_768, mask_BxS2_bf1)
    x, ctx_768, mask_BxS2_bf1 = _rec_inputs()

    def _L0_xattn_setup():
        import jax, jax.numpy as jnp
        import numpy as np
        DIM = 256
        CTX_DIM = 192
        HEADS = 16
        key = jax.random.key(seed)
        ks = jax.random.split(key, 7)
        B, N, M = (4, 1024, 64)
        x = jax.random.normal(ks[0], (B, N, DIM), dtype=jnp.float32)
        context = jax.random.normal(ks[1], (B, M, CTX_DIM), dtype=jnp.float32)
        context_mask = jnp.ones((B, M), dtype=bool)
        s_d = 1.0 / np.sqrt(DIM)
        s_c = 1.0 / np.sqrt(CTX_DIM)
        Wq = jax.random.normal(ks[2], (DIM, DIM), dtype=jnp.float32) * s_d
        Wk = jax.random.normal(ks[3], (CTX_DIM, DIM), dtype=jnp.float32) * s_c
        Wv = jax.random.normal(ks[4], (CTX_DIM, DIM), dtype=jnp.float32) * s_c
        Wo = jax.random.normal(ks[5], (DIM, DIM), dtype=jnp.float32) * s_d
        return {'x': x, 'context': context, 'context_mask': context_mask, 'Wq': Wq, 'Wk': Wk, 'Wv': Wv, 'Wo': Wo}
    _L0_xattn_all = _L0_xattn_setup()
    _L0_xattn_in = {k: v for k, v in _L0_xattn_all.items() if k in ('Wq', 'Wk', 'Wv', 'Wo')}
    del _L0_xattn_all

    def _L0_ffn_setup():
        import jax, jax.numpy as jnp
        import numpy as np
        B, S, D, H, E = (8, 512, 256, 1024, 16)
        key = jax.random.key(seed)
        ks = jax.random.split(key, 4)
        sd = 1.0 / np.sqrt(D).astype(np.float32)
        sh = 1.0 / np.sqrt(H).astype(np.float32)
        return {'x': jax.random.normal(ks[0], (B, S, D), jnp.float32), 'Wg': jax.random.normal(ks[1], (D, E), jnp.float32) * sd, 'bg': jnp.zeros((E,), jnp.float32), 'W1': jax.random.normal(ks[2], (E, D, H), jnp.float32) * sd, 'b1': jnp.zeros((E, H), jnp.float32), 'W2': jax.random.normal(ks[3], (E, H, D), jnp.float32) * sh, 'b2': jnp.zeros((E, D), jnp.float32)}
    _L0_ffn_all = _L0_ffn_setup()
    _L0_ffn_in = {k: v for k, v in _L0_ffn_all.items() if k in ('Wg', 'bg', 'W1', 'b1', 'W2', 'b2')}
    del _L0_ffn_all
    return {'x': x, 'ctx_768': ctx_768, 'mask_BxS2_bf1': mask_BxS2_bf1, 'L0_xattn_Wq': _L0_xattn_in['Wq'], 'L0_xattn_Wk': _L0_xattn_in['Wk'], 'L0_xattn_Wv': _L0_xattn_in['Wv'], 'L0_xattn_Wo': _L0_xattn_in['Wo'], 'L0_ffn_Wg': _L0_ffn_in['Wg'], 'L0_ffn_bg': _L0_ffn_in['bg'], 'L0_ffn_W1': _L0_ffn_in['W1'], 'L0_ffn_b1': _L0_ffn_in['b1'], 'L0_ffn_W2': _L0_ffn_in['W2'], 'L0_ffn_b2': _L0_ffn_in['b2']}

def reference(x, ctx_768, mask_BxS2_bf1, L0_xattn_Wq, L0_xattn_Wk, L0_xattn_Wv, L0_xattn_Wo, L0_ffn_Wg, L0_ffn_bg, L0_ffn_W1, L0_ffn_b1, L0_ffn_W2, L0_ffn_b2):
    import jax
    import jax.numpy as jnp

    def _L0_xattn_ref(x, context, context_mask, Wq, Wk, Wv, Wo):
        import jax, jax.numpy as jnp
        import numpy as np
        DIM = 256
        CTX_DIM = 192
        HEADS = 16
        B, N, _ = x.shape
        M = context.shape[1]
        hd = DIM // HEADS
        scale = hd ** (-0.5)
        q = (x @ Wq).reshape(B, N, HEADS, hd).transpose(0, 2, 1, 3)
        k = (context @ Wk).reshape(B, M, HEADS, hd).transpose(0, 2, 1, 3)
        v = (context @ Wv).reshape(B, M, HEADS, hd).transpose(0, 2, 1, 3)
        scores = jnp.einsum('bhid,bhjd->bhij', q, k) * scale
        max_neg = -jnp.finfo(scores.dtype).max
        scores = jnp.where(context_mask[:, None, None, :], scores, max_neg)
        attn = jax.nn.softmax(scores, axis=-1)
        out = jnp.einsum('bhij,bhjd->bhid', attn, v)
        out = out.transpose(0, 2, 1, 3).reshape(B, N, DIM)
        return out @ Wo

    def _L0_ffn_ref(x, Wg, bg, W1, b1, W2, b2):
        import jax, jax.numpy as jnp
        import numpy as np
        B, S, D, H, E = (8, 512, 256, 1024, 16)
        d = x.shape[-1]
        xf = x.reshape(-1, d)
        n_tok = xf.shape[0]
        n_exp = Wg.shape[1]
        cap = -(-n_tok // n_exp)
        score = jax.nn.softmax(xf @ Wg + bg, axis=-1)
        gate = jnp.max(score, axis=-1)
        idx = jnp.argmax(score, axis=-1)
        onehot = jax.nn.one_hot(idx, n_exp, dtype=jnp.int32)
        pos = jnp.sum((jnp.cumsum(onehot, axis=0) - 1) * onehot, axis=-1)
        keep = pos < cap
        safe_pos = jnp.where(keep, pos, cap - 1)
        buf = jnp.zeros((n_exp, cap, d), x.dtype).at[idx, safe_pos].add(jnp.where(keep[:, None], xf, 0.0))
        h = jax.nn.relu(jnp.einsum('ecd,edh->ech', buf, W1) + b1[:, None, :])
        y = jnp.einsum('ech,ehd->ecd', h, W2) + b2[:, None, :]
        out = y[idx, safe_pos] * gate[:, None]
        out = jnp.where(keep[:, None], out, 0.0)
        return out.reshape(x.shape)
    x = x + _L0_xattn_ref(_layernorm(x, axis=-1), ctx_768, mask_BxS2_bf1, L0_xattn_Wq, L0_xattn_Wk, L0_xattn_Wv, L0_xattn_Wo)
    x = x + _L0_ffn_ref(_layernorm(x, axis=-1), L0_ffn_Wg, L0_ffn_bg, L0_ffn_W1, L0_ffn_b1, L0_ffn_W2, L0_ffn_b2)
    return x

_drawn_inputs = setup_inputs


def setup_inputs(seed=0):
    import zlib

    import numpy as np

    out = dict(_drawn_inputs(seed))
    spreads = {'L0_ffn_bg': (0.0, 0.1), 'L0_ffn_b1': (0.0, 0.509), 'L0_ffn_b2': (0.0, 0.358)}
    factors = {}
    for name, (base, spread) in spreads.items():
        noise = np.random.default_rng([zlib.crc32(name.encode()), seed]).standard_normal(out[name].shape)
        drawn = base * np.exp(spread * noise) if base else spread * noise
        out[name] = jnp.asarray(drawn.astype(out[name].dtype))
    for name, factor in factors.items():
        out[name] = (out[name] * factor).astype(out[name].dtype)
    return out
```

```python
from contextlib import ExitStack

import concourse.bass as bass
from concourse import mybir

F32 = mybir.dt.float32
BF16 = mybir.dt.bfloat16
I32 = mybir.dt.int32
U8 = mybir.dt.uint8
ALU = mybir.AluOpType
ACT = mybir.ActivationFunctionType
AX_X = mybir.AxisListType.X

P = 128
B, S, D = 128, 128, 256
C = 192
CK = C // 2
H, HD = 16, 16
E, HID, CAP = 16, 1024, 1024
G = 4
NG = B // G
T = G * S
NT = B * S
DC = D // P
SCALE = float(HD) ** -0.5
EPS = 1e-5
BIG = 1e30
NOWHERE = float(4 * NT)
SLOTS = ((0, 0), (0, 1), (0, 2), (1, 0), (1, 1), (2, 0))
KROWS = len(SLOTS) * HD
VW = HD + 1
ROW = D + 4
MC = HID // P
NH = 2 * E
HS = CAP // 2


class Step:

    def __init__(self, c, j=None):
        self.c, self.j = c, j

    def has(self, d, n=NG):
        return self.j is not None or 0 <= self.c + d < n

    def n(self, per, d, k=0):
        const = per * (self.c + d) + k
        return const if self.j is None else self.j * (2 * per) + const

    def half(self, per, d, k=0):
        const = per * ((self.c + d) // 2) + k
        return const if self.j is None else self.j * per + const

    def par(self, d):
        return (self.c + d) % 2


def wait_apart(eng, sem, value):
    eng.wait_ge(sem, value)
    if not isinstance(value, int):
        eng.nop(nofuse=True)


class Chain:

    def __init__(self, eng, sem, per_loop=0):
        self.eng, self.sem, self.n, self.per_loop, self.j = eng, sem, 0, per_loop, None

    def link(self, ins):
        ins.then_inc(self.sem, 1)
        self.n += 1
        wait_apart(self.eng, self.sem, self.n if self.j is None else self.j * self.per_loop + self.n)

    def enter(self, j):
        self.j, self.n0 = j, self.n

    def leave(self, times):
        assert self.n - self.n0 == self.per_loop, (self.n - self.n0, self.per_loop)
        self.j, self.n = None, self.n0 + times * self.per_loop


def steps(eng, do, chain=None, first=-3, loop=(1, 14), last=NG):
    start, times = loop
    for c in range(first, start):
        do(Step(c))
    with eng.Fori(0, times) as j:
        if chain:
            chain.enter(j)
        do(Step(start, j))
        do(Step(start + 1, j))
        if chain:
            chain.leave(times)
    for c in range(start + 2 * times, last + 1):
        do(Step(c))


def attention_phase(nc, io, dr, sem):
    with ExitStack() as ctx:
        def sb(name, shape, dt=F32):
            return ctx.enter_context(nc.sbuf_tensor(name, shape, dt))

        def ps(name, shape, dt=F32):
            return ctx.enter_context(nc.psum_tensor(name, shape, dt))

        ident = sb("ident", [P, P])
        before = sb("before", [P, P], BF16)
        ones = sb("ones", [P, P], BF16)
        onesf = sb("onesf", [P, P])
        first_e = sb("first_e", [P, E])
        half_neg = sb("half_neg", [P, G])
        gate_bias = sb("gate_bias", [P, E])
        wq = sb("wq", [P, DC, D])
        wk = sb("wk", [CK, 2, D])
        wv = sb("wv", [CK, 2, D])
        wo = sb("wo", [P, DC, D])
        wg = sb("wg", [P, DC, P])
        maskrow = sb("maskrow", [B, S], BF16)
        anyrow = sb("anyrow", [B, 1])
        exp_scale = sb("exp_scale", [P, B])
        group_scale = [sb(f"group_scale{i}", [P, G]) for i in range(2)]
        empty_row = sb("empty_row", [P, ROW])
        x_in = [sb(f"x_in{i}", [P, G, D]) for i in range(2)]
        c_in = [sb(f"c_in{i}", [P, G, C]) for i in range(2)]
        xn = sb("xn", [P, G, D])
        xT = sb("xT", [P, DC, T])
        cT = [sb(f"cT{i}", [CK, 2, T]) for i in range(2)]
        parts = [sb(f"parts{i}", [P, DC, 3, T], BF16) for i in range(2)]
        rest = [sb(f"rest{i}", [P, T]) for i in range(2)]
        Qs = [sb(f"Qs{i}", [P, H, T], BF16) for i in range(2)]
        Ks = [sb(f"Ks{i}", [P, H, T], BF16) for i in range(2)]
        V = [sb(f"V{i}", [P, G, H * VW + 16]) for i in range(2)]
        M = sb("M", [P, G, H])
        Mparts = sb("Mparts", [H, 2, T], BF16)
        PT = [sb(f"PT{i}", [P, H, S]) for i in range(2)]
        OT = sb("OT", [P, G, S])
        On = sb("On", [P, H, HD])
        OnT = sb("OnT", [P, DC, S])
        inv = sb("inv", [P, H])
        xr = [sb(f"xr{i}", [P, G, ROW]) for i in range(2)]
        xn2 = sb("xn2", [P, G, D])
        x2T = sb("x2T", [P, DC, T])
        st1 = sb("st1", [P, 6])
        ag1 = sb("ag1", [P, G, 2])
        var1 = sb("var1", [P, G])
        rstd1 = sb("rstd1", [P, G])
        st2 = sb("st2", [P, 6])
        ag2 = sb("ag2", [P, G, 2])
        var2 = sb("var2", [P, G])
        lg = sb("lg", [P, G, E])
        lmax = sb("lmax", [P, G])
        hit = sb("hit", [P, G, E])
        best = sb("best", [P, G])
        onehot = sb("onehot", [P, G, E], BF16)
        expl = sb("expl", [P, G, E])
        count = sb("count", [P, E])
        seen = sb("seen", [P, E], BF16)
        seenf = sb("seenf", [P, E])
        posx = sb("posx", [P, G, E])
        pos = sb("pos", [P, G])
        over = sb("over", [P, G])
        slotf = sb("slotf", [P, G])
        esum = sb("esum", [P, G])
        sloti = [sb(f"sloti{i}", [P, G], I32) for i in range(2)]
        token = sb("token", [P, G])

        psA = [ps(f"psA{i}", [P, T]) for i in range(2)]
        psS1 = [ps(f"psS1{i}", [P, G, S]) for i in range(2)]
        psS2 = [ps(f"psS2{i}", [P, G, S]) for i in range(2)]
        psAV = ps("psAV", [P, G, S])
        psO = ps("psO", [P, T])

        x2d = io["x"].rearrange("b s d -> s b d")
        c2d = io["ctx_768"].rearrange("b s d -> s b d")
        out_sb = io["out"].rearrange("b s d -> s b d")

        weights_loaded = sem("weights_loaded")
        mask_loaded = sem("mask_loaded")
        maskrow_stored = sem("maskrow_stored")
        maskrow_ready = sem("maskrow_ready")
        rows_emptied = sem("rows_emptied")
        pool_const = sem("pool_const")
        pool_const2 = sem("pool_const2")
        dve_const = sem("dve_const")
        empty_ready = sem("empty_ready")
        any_ready = sem("any_ready")
        any_spread = sem("any_spread")
        x_loaded = [sem(f"x_loaded{i}") for i in range(2)]
        c_loaded = [sem(f"c_loaded{i}") for i in range(2)]
        xr_loaded = [sem(f"xr_loaded{i}") for i in range(2)]
        parts_stored = [sem(f"parts_stored{i}") for i in range(2)]
        stack_loaded = [sem(f"stack_loaded{i}") for i in range(2)]
        mrows_loaded = [sem(f"mrows_loaded{i}") for i in range(2)]
        x1_stored = [sem(f"x1_stored{i}") for i in range(2)]
        dispatched = [sem(f"dispatched{i}") for i in range(2)]
        mT_done, v_done, xT_done, cT_done, qk_done, x2T_done, lg_done, pos_done = (
            sem(x) for x in ("mT_done", "v_done", "xT_done", "cT_done", "qk_done", "x2T_done", "lg_done", "pos_done"))
        s1_done, s2_done, av_done, o_turned, on_turned, wo_done = (
            sem(x) for x in ("s1_done", "s2_done", "av_done", "o_turned", "on_turned", "wo_done"))
        v_kept, xT_kept, cT_kept, high_kept, x2T_kept, exp_done, ot_kept, onT_kept, expl_done = (
            sem(x) for x in ("v_kept", "xT_kept", "cT_kept", "high_kept", "x2T_kept", "exp_done", "ot_kept",
                             "onT_kept", "expl_done"))
        stats1, rest_ready, max_done, mparts_ready, norm_done, x1_done, stats2, lg_kept, oh_ready, route_ready, pos_kept = (
            sem(x) for x in ("stats1", "rest_ready", "max_done", "mparts_ready", "norm_done", "x1_done", "stats2",
                             "lg_kept", "oh_ready", "route_ready", "pos_kept"))
        scale_ready = sem("scale_ready")
        dve_chain = sem("dve_chain")
        xn_ready, low_ready, xn2_ready, row_ready = (sem(x) for x in ("xn_ready", "low_ready", "xn2_ready", "row_ready"))
        pool_chain = sem("pool_chain")

        block = ctx.enter_context(nc.Block())

        @block.sync
        def _(sp):
            sp.dma_start(x_in[0][:], x2d[:, 0:G, :]).then_inc(x_loaded[0], 16)
            sp.dma_start(c_in[0][:], c2d[:, 0:G, :]).then_inc(c_loaded[0], 16)
            sp.dma_start(xT[:, :, 0:D], io["L0_xattn_Wq"].rearrange("(c p) n -> p c n", p=P)).then_inc(weights_loaded, 16)
            sp.dma_start(cT[0][:, :, 0:D], io["L0_xattn_Wk"].rearrange("(c p) n -> p c n", p=CK)).then_inc(weights_loaded, 16)
            sp.dma_start(wv[:], io["L0_xattn_Wv"].rearrange("(c p) n -> p c n", p=CK)).then_inc(weights_loaded, 16)
            sp.dma_start(wo[:], io["L0_xattn_Wo"].rearrange("(c p) n -> p c n", p=P)).then_inc(weights_loaded, 16)
            sp.dma_start(gate_bias[:], io["L0_ffn_bg"].rearrange("(a n) -> a n", a=1).broadcast_to([P, E])).then_inc(weights_loaded, 16)
            sp.dma_start(lg[:, 0:DC, :], io["L0_ffn_Wg"].rearrange("(c p) n -> p c n", p=P)).then_inc(weights_loaded, 16)
            sp.dma_start(M[:, :, :].rearrange("p g h -> p (g h)").bitcast(U8)[:, 0:S], io["mask_BxS2_bf1"]).then_inc(mask_loaded, 16)
            wait_apart(sp, empty_ready, 1)
            rows = dr["rows"].rearrange("(p r) n -> p r n", p=P)
            sp.dma_start(rows, empty_row[:].rearrange("p (r n) -> p r n", r=1).broadcast_to([P, NT // P, ROW])).then_inc(rows_emptied, 16)
            wait_apart(sp, maskrow_ready, 1)
            sp.dma_start(dr["maskrow"], maskrow[:]).then_inc(maskrow_stored, 16)
            wait_apart(sp, maskrow_stored, 16)

            def step(st):
                if st.has(0):
                    p = st.par(0)
                    wait_apart(sp, mparts_ready, st.n(1, 0, 1))
                    for i in range(2):
                        sp.dma_start(Qs[p][KROWS + 1 + i:KROWS + 2 + i, :, :], Mparts[:, i, :]).then_inc(mrows_loaded[p], 16)
                if st.has(1):
                    p = st.par(1)
                    wait_apart(sp, parts_stored[p], st.half(64, 1, 64))
                    if st.has(-1):
                        wait_apart(sp, s2_done, st.n(4 * G, 0))
                    for i, (a, b) in enumerate(SLOTS):
                        sp.dma_start(Qs[p][i * HD:(i + 1) * HD, :, :],
                                     dr["qparts"][p, a].rearrange("(d h) t -> d h t", h=H)).then_inc(stack_loaded[p], 16)
                    for r0, n in ((0, 3), (3, 2), (5, 1)):
                        sp.dma_start(Ks[p][r0 * HD:(r0 + n) * HD, :, :],
                                     dr["kparts"][p, 0:n].rearrange("a (d h) t -> (a d) h t", h=H)).then_inc(stack_loaded[p], 16)
                    row = dr["maskrow"].rearrange("(g b) s -> g (b s)", b=G)[st.n(1, 1) if st.j is None else bass.ds(st.n(1, 1), 1)]
                    row = row.rearrange("(a t) -> a t", a=1) if st.j is None else row
                    sp.dma_start(Ks[p][KROWS:KROWS + 1, :, :],
                                 row.rearrange("a (h t) -> a h t", h=1).broadcast_to([1, H, T])).then_inc(stack_loaded[p], 16)
                if st.has(-1):
                    p = st.par(-1)
                    wait_apart(sp, x1_done, st.n(G, 0))
                    sp.dma_start(out_sb[:, bass.ds(st.n(G, -1), G), :], xr[p][:, :, 0:D]).then_inc(x1_stored[p], 16)
                if st.has(2):
                    p = st.par(2)
                    if st.has(0):
                        wait_apart(sp, stack_loaded[p], st.half(160, 0, 160))
                    for i in range(2 * DC):
                        name, c = ("qparts", "kparts")[i // DC], i % DC
                        wait_apart(sp, low_ready, st.n(2 * DC, 2, i + 1))
                        sp.dma_start(dr[name][p, :, c * P:(c + 1) * P, :].rearrange("a r t -> r a t"),
                                     parts[i // DC][:, c, :, :]).then_inc(parts_stored[p], 16)
                if st.has(3) and not (st.j is None and st.c == -3):
                    p = st.par(3)
                    if st.has(1):
                        wait_apart(sp, xn_ready, st.n(1, 2))
                        wait_apart(sp, cT_done, st.n(2, 2))
                    sp.dma_start(x_in[p][:], x2d[:, bass.ds(st.n(G, 3), G), :]).then_inc(x_loaded[p], 16)
                    sp.dma_start(c_in[p][:], c2d[:, bass.ds(st.n(G, 3), G), :]).then_inc(c_loaded[p], 16)
                if st.has(1):
                    p = st.par(1)
                    if st.has(-1):
                        wait_apart(sp, x1_stored[p], st.half(16, -1, 16))
                        wait_apart(sp, dispatched[p], st.half(16 * G, -1, 16 * G))
                    sp.dma_start(xr[p][:, :, 0:D], x2d[:, bass.ds(st.n(G, 1), G), :]).then_inc(xr_loaded[p], 16)

            steps(sp, step)
            for p in range(2):
                wait_apart(sp, x1_stored[p], 16 * NG // 2)
                wait_apart(sp, dispatched[p], 16 * G * NG // 2)

        @block.gpsimd
        def _(pool):
            nc.gpsimd.memset(ident[:], 0.0).then_inc(pool_const, 1)
            nc.gpsimd.memset(before[:], 0.0).then_inc(pool_const, 1)
            nc.gpsimd.memset(ones[:], 1.0).then_inc(pool_const, 1)
            nc.gpsimd.memset(onesf[:], 1.0).then_inc(pool_const, 1)
            nc.gpsimd.memset(half_neg[:], -0.5).then_inc(pool_const, 1)
            nc.gpsimd.iota(first_e[:], pattern=[[-1, E]], base=E, channel_multiplier=0,
                           allow_small_or_imprecise_dtypes=True).then_inc(pool_const, 1)
            nc.gpsimd.iota(token[:], pattern=[[S, G]], base=0, channel_multiplier=1,
                           allow_small_or_imprecise_dtypes=True).then_inc(pool_const, 1)
            wait_apart(pool, pool_const, 7)
            nc.gpsimd.affine_select(out=ident[:], in_=ident[:], compare_op=ALU.not_equal, fill=1.0, base=0,
                                    pattern=[[-1, P]], channel_multiplier=1).then_inc(pool_const2, 1)
            nc.gpsimd.affine_select(out=before[:], in_=before[:], compare_op=ALU.is_ge, fill=1.0, base=0,
                                    pattern=[[-1, P]], channel_multiplier=1).then_inc(pool_const2, 1)
            chain = Chain(pool, pool_chain, per_loop=4)

            def step(st):
                if st.has(-1):
                    p = st.par(-1)
                    wait_apart(pool, stats2, st.n(1, 0))
                    if st.has(-2):
                        wait_apart(pool, x2T_done, st.n(2, -1))
                    chain.link(nc.gpsimd.tensor_scalar(var2[:], ag2[:, :, 1], EPS, None, ALU.add))
                    nc.gpsimd.tensor_copy(xr[p][:, :, D + 2], ag2[:, :, 0])
                    chain.link(nc.gpsimd.tensor_tensor(xr[p][:, :, D + 3], var2[:], half_neg[:], ALU.pow))
                    for b in range(G):
                        last = nc.gpsimd.tensor_scalar(xn2[:, b, :], xr[p][:, b, 0:D], xr[p][:, b, D + 2:D + 3],
                                                       xr[p][:, b, D + 3:D + 4], ALU.subtract, ALU.mult)
                    last.then_inc(xn2_ready, 1)
                if st.has(2):
                    for i in range(2 * DC):
                        wait_apart(pool, rest_ready, st.n(2 * DC, 2, i + 1))
                        part, c = parts[i // DC], i % DC
                        nc.gpsimd.tensor_copy(part[:, c, 1, :], rest[i % 2][:]).then_inc(row_ready, 1)
                        wait_apart(pool, row_ready, st.n(2 * DC, 2, i + 1))
                        nc.gpsimd.tensor_tensor(part[:, c, 2, :], rest[i % 2][:], part[:, c, 1, :],
                                                ALU.subtract).then_inc(low_ready, 1)
                if st.has(-1):
                    p = st.par(-1)
                    wait_apart(pool, rows_emptied, 16)
                    wait_apart(pool, route_ready, st.n(1, 0))
                    for b in range(G):
                        nc.gpsimd.indirect_dma_start(
                            out=dr["rows"], out_offset=bass.IndirectOffsetOnAxis(ap=sloti[p][:, b:b + 1], axis=0),
                            in_=xr[p][:, b, :], in_offset=None, bounds_check=NT - 1, oob_is_err=False,
                        ).then_inc(dispatched[p], 16)
                if st.has(3):
                    p = st.par(3)
                    wait_apart(pool, stats1, st.n(1, 4))
                    if st.has(2):
                        wait_apart(pool, xT_done, st.n(2, 3))
                    chain.link(nc.gpsimd.tensor_scalar(var1[:], ag1[:, :, 1], EPS, None, ALU.add))
                    chain.link(nc.gpsimd.tensor_tensor(rstd1[:], var1[:], half_neg[:], ALU.pow))
                    for b in range(G):
                        last = nc.gpsimd.tensor_scalar(xn[:, b, :], x_in[p][:, b, :], ag1[:, b, 0:1],
                                                       rstd1[:, b:b + 1], ALU.subtract, ALU.mult)
                    last.then_inc(xn_ready, 1)

            chain.per_loop = 8
            wait_apart(pool, pool_const2, 2)
            steps(pool, step, chain)

        @block.scalar
        def _(act):
            def on_turned_back(st, d, b):
                act.wait_ge(on_turned, st.n(G, d, b + 1))
                nc.scalar.copy(OnT[:].rearrange("p c s -> p (c s)"), psO[:, 0:D]).then_inc(onT_kept, 1)

            def step(st):
                if st.has(1):
                    p = st.par(1)
                    for i in range(2):
                        act.wait_ge(v_done, st.n(2, 1, i + 1))
                        if i == 0 and st.has(-1):
                            act.wait_ge(av_done, st.n(G, 0))
                        if i == 0:
                            act.wait_ge(dve_const, 1)
                        dst = V[p][:, 2 * i:2 * i + 2, 0:H * VW].rearrange("p b (h w) -> p b h w", w=VW)
                        for b in range(2):
                            last = nc.scalar.copy(dst[:, b, :, 0:HD], psA[1 - i][:, b * D:(b + 1) * D].rearrange("p (h w) -> p h w", w=HD))
                        last.then_inc(v_kept, 1)
                if st.has(-1):
                    on_turned_back(st, -1, G - 1)
                if st.has(2):
                    p = st.par(2)
                    for c in range(DC):
                        act.wait_ge(xT_done, st.n(2, 2, c + 1))
                        if c == 0:
                            act.wait_ge(dve_const, 1)
                            if st.has(1):
                                act.wait_ge(qk_done, st.n(4, 2))
                        nc.scalar.copy(xT[:, c, :], psA[1 - c][:]).then_inc(xT_kept, 1)
                    for c in range(2):
                        act.wait_ge(cT_done, st.n(2, 2, c + 1))
                        nc.scalar.copy(cT[p][:, c, :], psA[1 - c][0:CK, :]).then_inc(cT_kept, 1)
                    for i in range(2 * DC):
                        act.wait_ge(qk_done, st.n(4, 2, i + 1))
                        if i == 0 and st.has(1):
                            act.wait_ge(parts_stored[st.par(1)], st.half(64, 1, 64))
                        nc.scalar.copy(parts[i // DC][:, i % DC, 0, :], psA[1 - i % 2][:]).then_inc(high_kept, 1)
                if st.has(-1):
                    for c in range(DC):
                        act.wait_ge(x2T_done, st.n(2, -1, c + 1))
                        if c == 0 and st.has(-2):
                            act.wait_ge(lg_done, st.n(1, -1))
                        nc.scalar.copy(x2T[:, c, :], psA[1 - c][:]).then_inc(x2T_kept, 1)
                    act.wait_ge(oh_ready, st.n(1, 0))
                    nc.scalar.activation(expl[:], lg[:], ACT.Exp).then_inc(expl_done, 1)
                if st.has(0):
                    for t in range(G + 1):
                        for k in range(4):
                            if t < G:
                                act.wait_ge(s2_done, st.n(16, 0, 4 * t + k + 1))
                                if k == 0 and (t >= 2 or st.has(-1)):
                                    act.wait_ge(av_done, st.n(G, 0, t - 1))
                                if t == 0 and k == 0:
                                    act.wait_ge(scale_ready, st.n(1, 0, 1))
                                nc.scalar.activation(
                                    PT[t % 2][:, 4 * k:4 * k + 4, :], psS2[k % 2][:], ACT.Exp,
                                    scale=group_scale[st.par(0)][:, t:t + 1]).then_inc(exp_done, 1)
                            if k == 1 and t >= 2:
                                on_turned_back(st, 0, t - 2)
                        if t >= 1:
                            act.wait_ge(av_done, st.n(G, 0, t))
                            nc.scalar.copy(OT[:], psAV[:]).then_inc(ot_kept, 1)

            steps(act, step)

        @block.vector
        def _(dve):
            chain = Chain(dve, dve_chain)
            nc.vector.memset(empty_row[:], 0.0)
            chain.link(nc.vector.memset(seenf[:], 0.0))
            nc.vector.memset(empty_row[:, D + 1:D + 2], NOWHERE).then_inc(empty_ready, 1)
            nc.vector.memset(seen[:], 0.0)
            for p in range(2):
                nc.vector.memset(V[p][:], 1.0)
                nc.vector.memset(Qs[p][KROWS:KROWS + 3, :, :], 1.0)
                nc.vector.memset(Ks[p][KROWS:KROWS + 3, :, :], 1.0)
            nc.vector.memset(wg[:], 0.0)
            dve.wait_ge(mask_loaded, 16)
            mask8 = M[:, :, :].rearrange("p g h -> p (g h)").bitcast(U8)[:, 0:S]
            chain.link(nc.vector.tensor_copy(PT[0][:, 0, :], mask8))
            nc.vector.tensor_scalar(maskrow[:], PT[0][:, 0, :], 1.0, BIG, ALU.subtract, ALU.mult).then_inc(maskrow_ready, 1)
            chain.link(nc.vector.tensor_reduce(anyrow[:], PT[0][:, 0, :], AX_X, ALU.max))
            dve.wait_ge(pool_const2, 2)
            nc.vector.tensor_scalar(PT[0][:, 1, :], ident[:], anyrow[:, 0:1], SCALE, ALU.mult, ALU.mult).then_inc(any_ready, 1)
            dve.wait_ge(weights_loaded, 96)
            for c in range(DC):
                nc.vector.tensor_copy(wq[:, c, :].rearrange("p (d h) -> p d h", h=H),
                                      xT[:, c, 0:D].rearrange("p (h d) -> p d h", d=HD))
                nc.vector.tensor_copy(wk[:, c, :].rearrange("p (d h) -> p d h", h=H),
                                      cT[0][:, c, 0:D].rearrange("p (h d) -> p d h", d=HD))
            chain.link(nc.vector.tensor_copy(wg[:, :, 0:E], lg[:, 0:DC, :]))
            dve.sem_inc(dve_const, 1)
            dve.wait_ge(any_spread, 1)
            nc.vector.tensor_copy(exp_scale[:], psS2[0][:, 0, :]).then_inc(any_spread, 1)
            dve.wait_ge(any_spread, 2)

            def norm(st, d, b):
                dve.wait_ge(o_turned, st.n(G, d, b + 1))
                o = psO[:].rearrange("p (h w) -> p h w", w=32)
                chain.link(nc.vector.reciprocal(inv[:], o[:, :, HD]))
                nc.vector.tensor_tensor(On[:], o[:, :, 0:HD], inv[:].rearrange("p (h w) -> p h w", w=1).broadcast_to([P, H, HD]),
                                        ALU.mult).then_inc(norm_done, 1)

            def residual(st, d, b):
                p = st.par(d)
                dve.wait_ge(wo_done, st.n(G, d, b + 1))
                if b == 0:
                    dve.wait_ge(xr_loaded[p], st.half(16, d, 16))
                nc.vector.tensor_tensor(xr[p][:, b, 0:D], psO[:, 0:D], xr[p][:, b, 0:D], ALU.add).then_inc(x1_done, 1)
                dve.wait_ge(x1_done, st.n(G, d, b + 1))
                chain.link(nc.vector.bn_stats(st2[:], xr[p][:, b, 0:D]))
                if b == 0 and st.has(d - 1):
                    wait_apart(dve, xn2_ready, st.n(1, d))
                last = nc.vector.bn_aggr(ag2[:, b, :], st2[:])
                if b == G - 1:
                    last.then_inc(stats2, 1)
                else:
                    chain.link(last)

            def step(st):
                if st.has(0):
                    if st.has(-2):
                        wait_apart(dve, exp_done, st.n(16, -1))
                    nc.vector.tensor_copy(group_scale[st.par(0)][:], exp_scale[:, bass.ds(st.n(G, 0), G)]).then_inc(scale_ready, 1)
                    dve.wait_ge(mT_done, st.n(1, 0, 1))
                    if st.has(-1):
                        dve.wait_ge(mrows_loaded[st.par(-1)], st.half(32, -1, 32))
                    chain.link(nc.vector.tensor_scalar(Mparts[:, 0, :], psA[0][0:H, :], -1.0, None, ALU.mult))
                    nc.vector.scalar_tensor_tensor(out=Mparts[:, 1, :], in0=psA[0][0:H, :], scalar=-1.0,
                                                   in1=Mparts[:, 0, :], op0=ALU.mult, op1=ALU.subtract).then_inc(mparts_ready, 1)
                if st.has(-1):
                    norm(st, -1, G - 1)
                    residual(st, -1, G - 1)
                if st.has(2):
                    for i in range(2 * DC):
                        dve.wait_ge(high_kept, st.n(4, 2, i + 1))
                        if i >= 2 or st.has(1):
                            dve.wait_ge(low_ready, st.n(4, 2, i - 1))
                        nc.vector.tensor_tensor(rest[i % 2][:], psA[1 - i % 2][:], parts[i // DC][:, i % DC, 0, :],
                                                ALU.subtract).then_inc(rest_ready, 1)
                if st.has(-1):
                    p = st.par(-1)

                    def spread(a):
                        return a[:].rearrange("p (g e) -> p g e", e=1).broadcast_to([P, G, E])

                    dve.wait_ge(lg_done, st.n(1, 0))
                    nc.vector.tensor_tensor(lg[:], psA[1][:].rearrange("p (g e) -> p g e", e=P)[:, :, 0:E],
                                            gate_bias[:].rearrange("p (g e) -> p g e", g=1).broadcast_to([P, G, E]),
                                            ALU.add).then_inc(lg_kept, 1)
                    dve.wait_ge(lg_kept, st.n(1, 0))
                    chain.link(nc.vector.tensor_reduce(lmax[:], lg[:], AX_X, ALU.max))
                    chain.link(nc.vector.tensor_tensor(hit[:], lg[:], spread(lmax), ALU.is_equal))
                    chain.link(nc.vector.tensor_tensor(hit[:], hit[:], first_e[:].rearrange("p (g e) -> p g e", g=1).broadcast_to([P, G, E]), ALU.mult))
                    chain.link(nc.vector.tensor_reduce(best[:], hit[:], AX_X, ALU.max))
                    chain.link(nc.vector.tensor_tensor(onehot[:], hit[:], spread(best), ALU.is_equal))
                    nc.vector.tensor_tensor(lg[:], lg[:], spread(lmax), ALU.subtract).then_inc(oh_ready, 1)
                    dve.wait_ge(pos_done, st.n(1, 0))
                    nc.vector.tensor_tensor(posx[:], psA[0][:, 0:G * E].rearrange("p (g e) -> p g e", e=E), onehot[:],
                                            ALU.mult).then_inc(pos_kept, 1)
                    dve.wait_ge(pos_kept, st.n(1, 0))
                    chain.link(nc.vector.tensor_reduce(count[:], onehot[:].rearrange("p g e -> p e g"), AX_X, ALU.add))
                    chain.link(nc.vector.tensor_tensor(seenf[:], seenf[:], count[:], ALU.add))
                    nc.vector.tensor_copy(seen[:], seenf[:])
                    chain.link(nc.vector.tensor_reduce(pos[:], posx[:], AX_X, ALU.add))
                    nc.vector.tensor_scalar(over[:], pos[:], float(CAP), NOWHERE, ALU.is_ge, ALU.mult)
                    chain.link(nc.vector.tensor_scalar(slotf[:], best[:], -float(CAP), float(CAP * E), ALU.mult, ALU.add))
                    chain.link(nc.vector.tensor_tensor(slotf[:], slotf[:], pos[:], ALU.add))
                    nc.vector.tensor_tensor(sloti[p][:], slotf[:], over[:], ALU.add)
                    dve.wait_ge(expl_done, st.n(1, 0))
                    chain.link(nc.vector.tensor_reduce(esum[:], expl[:], AX_X, ALU.add))
                    nc.vector.reciprocal(xr[p][:, :, D], esum[:])
                    chain.link(nc.vector.tensor_copy(xr[p][:, :, D + 1], token[:]))
                    nc.vector.tensor_scalar(token[:], token[:], float(T), None, ALU.add).then_inc(route_ready, 1)
                    dve.wait_ge(route_ready, st.n(1, 0))
                for t in range(G + 1):
                    if st.has(0) and t >= 2:
                        norm(st, 0, t - 2)
                    if st.has(1) and t < G:
                        for k in range(4):
                            dve.wait_ge(s1_done, st.n(16, 1, 4 * t + k + 1))
                            if t == 0 and k == 0 and st.has(0):
                                dve.wait_ge(mT_done, st.n(1, 1))
                            nc.vector.tensor_reduce(M[:, t, 4 * k:4 * k + 4], psS1[k % 2][:], AX_X, ALU.max).then_inc(max_done, 1)
                    if st.has(3) and t < G:
                        p = st.par(3)
                        if t == 0:
                            dve.wait_ge(x_loaded[p], st.half(16, 3, 16))
                            if st.has(2):
                                dve.wait_ge(xn_ready, st.n(1, 3))
                        chain.link(nc.vector.bn_stats(st1[:], x_in[p][:, t, :]))
                        last = nc.vector.bn_aggr(ag1[:, t, :], st1[:])
                        if t == G - 1:
                            last.then_inc(stats1, 1)
                        else:
                            chain.link(last)
                    if st.has(0) and t >= 2:
                        residual(st, 0, t - 2)

            chain.per_loop = 2 * (1 + G + (2 * G - 1) + 12 + (2 * G - 1))
            steps(dve, step, chain)

        @block.tensor
        def _(pe):
            pe.wait_ge(any_ready, 1)
            nc.tensor.matmul(psS2[0][:, 0, :], onesf[:], PT[0][:, 1, :], start=True, stop=True).then_inc(any_spread, 1)
            pe.wait_ge(dve_const, 1)
            pe.wait_ge(any_spread, 2)

            def turn_o(st, d, b):
                pe.wait_ge(ot_kept, st.n(G, d, b + 1))
                if b >= 1 or st.has(d - 1):
                    pe.wait_ge(x1_done, st.n(G, d, b))
                for g in range(4):
                    last = nc.tensor.transpose(psO[:, g * P:(g + 1) * P], OT[:, g, :], ident[:])
                last.then_inc(o_turned, 1)

            def turn_on(st, d, b):
                pe.wait_ge(norm_done, st.n(G, d, b + 1))
                for c in range(DC):
                    last = nc.tensor.transpose(psO[:, c * P:(c + 1) * P], On[:, c * 8:(c + 1) * 8, :].rearrange("p h w -> p (h w)"), ident[:])
                last.then_inc(on_turned, 1)

            def project(st, d, b):
                pe.wait_ge(onT_kept, st.n(G, d, b + 1))
                for c in range(DC):
                    last = nc.tensor.matmul(psO[:, 0:D], OnT[:, c, :], wo[:, c, :], start=(c == 0), stop=(c == DC - 1))
                last.then_inc(wo_done, 1)

            def step(st):
                if st.has(0):
                    pe.wait_ge(max_done, st.n(16, 1))
                    if st.has(1):
                        pe.wait_ge(rest_ready, st.n(4, 2))
                    if st.has(-2):
                        pe.wait_ge(pos_kept, st.n(1, -1))
                    for b in range(G):
                        last = nc.tensor.transpose(psA[0][0:H, b * P:(b + 1) * P], M[:, b, :], ident[:])
                    last.then_inc(mT_done, 1)
                if st.has(-1):
                    turn_o(st, -1, G - 1)
                if st.has(1):
                    p = st.par(1)
                    pe.wait_ge(rest_ready, st.n(4, 2))
                    for i in range(2):
                        if i == 0 and st.has(-2):
                            pe.wait_ge(lg_kept, st.n(1, -1))
                        if i == 1 and st.has(0):
                            pe.wait_ge(mparts_ready, st.n(1, 0, 1))
                        for b in range(2):
                            for c in range(2):
                                at = (2 * i + b) * S
                                last = nc.tensor.matmul(psA[1 - i][:, b * D:(b + 1) * D], cT[p][:, c, at:at + S], wv[:, c, :],
                                                        start=(c == 0), stop=(c == 1))
                        last.then_inc(v_done, 1)
                if st.has(-1):
                    turn_on(st, -1, G - 1)
                if st.has(2):
                    pe.wait_ge(xn_ready, st.n(1, 2, 1))
                    for c in range(DC):
                        if st.has(1):
                            pe.wait_ge(v_kept, st.n(2, 1, c + 1))
                        for b in range(G):
                            last = nc.tensor.transpose(psA[1 - c][:, b * P:(b + 1) * P], xn[:, b, c * P:(c + 1) * P], ident[:])
                        last.then_inc(xT_done, 1)
                if st.has(-1):
                    project(st, -1, G - 1)
                if st.has(2):
                    p = st.par(2)
                    pe.wait_ge(c_loaded[p], st.half(16, 2, 16))
                    for c in range(2):
                        pe.wait_ge(xT_kept, st.n(2, 2, c + 1))
                        for b in range(G):
                            last = nc.tensor.transpose(psA[1 - c][0:CK, b * P:(b + 1) * P], c_in[p][:, b, c * CK:(c + 1) * CK], ident[:])
                        last.then_inc(cT_done, 1)
                    for i in range(2 * DC):
                        if i < 2:
                            pe.wait_ge(cT_kept, st.n(2, 2, i + 1))
                        else:
                            pe.wait_ge(rest_ready, st.n(4, 2, i - 1))
                        m = (i % DC) * P
                        for c in range(2):
                            w, a = ((wq, xT), (wk, cT[p]))[i // DC]
                            last = nc.tensor.matmul(psA[1 - i % 2][:], w[:, c, m:m + P], a[:, c, :], start=(c == 0), stop=(c == 1))
                        last.then_inc(qk_done, 1)
                if st.has(-1):
                    pe.wait_ge(xn2_ready, st.n(1, 0))
                    if st.has(2):
                        pe.wait_ge(rest_ready, st.n(4, 3))
                    if st.has(1):
                        pe.wait_ge(v_kept, st.n(2, 2))
                    if st.has(0):
                        pe.wait_ge(mparts_ready, st.n(1, 0, 1))
                    if st.has(-2):
                        pe.wait_ge(pos_kept, st.n(1, -1))
                        pe.wait_ge(lg_kept, st.n(1, -1))
                    for c in range(DC):
                        for b in range(G):
                            last = nc.tensor.transpose(psA[1 - c][:, b * P:(b + 1) * P], xn2[:, b, c * P:(c + 1) * P], ident[:])
                        last.then_inc(x2T_done, 1)
                    pe.wait_ge(x2T_kept, st.n(2, 0))
                    for b in range(G):
                        for c in range(DC):
                            last = nc.tensor.matmul(psA[1][:, b * P:(b + 1) * P], x2T[:, c, b * P:(b + 1) * P], wg[:, c, :],
                                                    start=(c == 0), stop=(c == DC - 1))
                    last.then_inc(lg_done, 1)
                    pe.wait_ge(oh_ready, st.n(1, 0))
                    if st.has(-2):
                        pe.wait_ge(route_ready, st.n(1, -1))
                    oh = onehot[:].rearrange("p g e -> p (g e)")
                    nc.tensor.matmul(psA[0][:, 0:G * E], before[:], oh, start=True, stop=False)
                    for b in range(G - 1):
                        for b2 in range(b + 1, G):
                            nc.tensor.matmul(psA[0][:, b2 * E:(b2 + 1) * E], ones[:], onehot[:, b, :], start=False, stop=False,
                                             skip_group_check=True)
                    last = nc.tensor.matmul(psA[0][:, 0:G * E], ones[:],
                                            seen[:].rearrange("p (g e) -> p g e", g=1).broadcast_to([P, G, E]),
                                            start=False, stop=True)
                    last.then_inc(pos_done, 1)

                for t in range(G + 1):
                    do_s2 = st.has(0) and t < G
                    do_av = st.has(0) and t >= 1
                    do_s1 = st.has(1) and t < G
                    do_o = st.has(0) and t >= 2
                    if do_s1 and t == 0:
                        pe.wait_ge(stack_loaded[st.par(1)], st.half(160, 1, 160))
                    if do_s2 and t == 0:
                        pe.wait_ge(mrows_loaded[st.par(0)], st.half(32, 0, 32))
                    if do_o:
                        turn_o(st, 0, t - 2)
                    for k in range(4):
                        if do_s2:
                            if t or k >= 2 or st.has(-1):
                                pe.wait_ge(exp_done, st.n(16, 0, 4 * t + k - 1))
                            p, r = st.par(0), KROWS + 3
                            for i in range(4):
                                h = 4 * k + i
                                last = nc.tensor.matmul(psS2[k % 2][:, i, :], Ks[p][0:r, h, t * S:(t + 1) * S],
                                                        Qs[p][0:r, h, t * S:(t + 1) * S], start=True, stop=True)
                            last.then_inc(s2_done, 1)
                        if do_av:
                            pe.wait_ge(exp_done, st.n(16, 0, 4 * (t - 1) + k + 1))
                            if t == 1 and k == 0:
                                pe.wait_ge(v_kept, st.n(2, 1))
                            if k == 0 and (t >= 2 or st.has(-1)):
                                pe.wait_ge(ot_kept, st.n(G, 0, t - 1))
                            for i in range(4):
                                h = 4 * k + i
                                last = nc.tensor.matmul(psAV[32 * i:32 * i + 32, k, :], V[st.par(0)][:, t - 1, h * VW:h * VW + 32],
                                                        PT[(t - 1) % 2][:, h, :], start=True, stop=True)
                            if k == 3:
                                last.then_inc(av_done, 1)
                        if do_s1:
                            if t or k >= 2 or st.has(0):
                                pe.wait_ge(max_done, st.n(16, 1, 4 * t + k - 1))
                            p, r = st.par(1), KROWS + 1
                            for i in range(4):
                                h = 4 * k + i
                                last = nc.tensor.matmul(psS1[k % 2][:, i, :], Qs[p][0:r, h, t * S:(t + 1) * S],
                                                        Ks[p][0:r, h, t * S:(t + 1) * S], start=True, stop=True)
                            last.then_inc(s1_done, 1)
                        if do_o and k == 1:
                            turn_on(st, 0, t - 2)
                    if do_o:
                        project(st, 0, t - 2)

            steps(pe, step)


def expert_phase(nc, io, dr, sem):
    with ExitStack() as ctx:
        def sb(name, shape, dt=F32):
            return ctx.enter_context(nc.sbuf_tensor(name, shape, dt))

        def ps(name, shape, dt=F32):
            return ctx.enter_context(nc.psum_tensor(name, shape, dt))

        NS = HS // P
        ident = sb("ident2", [P, P])
        b1in = sb("b1in", [P, P])
        b1T = sb("b1T", [P, E * MC])
        bias = [sb(f"bias{i}", [P, MC]) for i in range(2)]
        w1 = [sb(f"w1_{i}", [P, DC, HID]) for i in range(2)]
        w2 = [sb(f"w2_{i}", [P, MC, D]) for i in range(2)]
        b2 = [sb(f"b2_{i}", [P, D]) for i in range(2)]
        rows = [sb(f"rows{i}", [P, NS, ROW]) for i in range(2)]
        ids = [sb(f"ids{i}", [P, NS], I32) for i in range(2)]
        xe = sb("xe", [P, NS, D])
        xeT = [sb(f"xeT{i}", [P, DC, HS]) for i in range(2)]
        h = [sb(f"h{i}", [P, MC, HS]) for i in range(2)]
        y = [sb(f"y{i}", [P, D]) for i in range(2)]
        yo = [sb(f"yo{i}", [P, NS, D]) for i in range(2)]
        psT = [ps(f"psT{i}", [P, HS]) for i in range(2)]
        psH = [ps(f"psH{i}", [P, HS]) for i in range(4)]
        psY = [ps(f"psY{i}", [P, HS]) for i in range(2)]

        ident_zero, ident_ready, b1_loaded, b1_turned, b1_kept = (
            sem(x) for x in ("ident_zero", "ident_ready", "b1_loaded", "b1_turned", "b1_kept"))
        rows_loaded = [sem(f"rows_loaded{i}") for i in range(2)]
        w_loaded = [sem(f"w_loaded{i}") for i in range(2)]
        scattered = [sem(f"scattered{i}") for i in range(2)]
        bias_ready = sem("bias_ready")
        xe_ready, ids_ready, xeT_done, xeT_kept, h_done, h_kept, y_done, y_kept, out_ready = (
            sem(x) for x in ("xe_ready", "ids_ready", "xeT_done", "xeT_kept", "h_done", "h_kept", "y_done", "y_kept",
                             "out_ready"))
        rows_in = dr["rows"].rearrange("(q s p) n -> q p s n", p=P, s=NS)
        out2d = io["out"].rearrange("b s d -> (b s) d")

        class Half(Step):

            def n(self, per, d, k=0):
                const = per * (self.c + d) + k
                return const if self.j is None else self.j * (4 * per) + const

            def half(self, per, d, k=0):
                const = per * ((self.c + d) // 2) + k
                return const if self.j is None else self.j * (2 * per) + const

            def expert(self, per, d, k=0):
                return self.half(per, d, k)

            def quarter(self, per, d, k=0):
                const = per * ((self.c + d) // 4) + k
                return const if self.j is None else self.j * per + const

            def expar(self, d):
                return (self.c + d) // 2 % 2

        def halves(eng, do, first=-1):
            for c in range(first, 4):
                do(Half(c))
            with eng.Fori(0, NH // 4 - 2) as j:
                for c in range(4):
                    do(Half(4 + c, j))
            for c in range(NH - 4, NH):
                do(Half(c))

        block = ctx.enter_context(nc.Block())

        @block.sync
        def _(sp):
            sp.dma_start(b1in[:], io["L0_ffn_b1"].rearrange("e (m p) -> (e m) p", p=P)).then_inc(b1_loaded, 16)

            def load_expert(st, d):
                q = st.expar(d)
                e = bass.ds(st.expert(1, d), 1)
                sp.dma_start(w1[q][:], io["L0_ffn_W1"][e].rearrange("e (c p) n -> p (e c) n", p=P)).then_inc(w_loaded[q], 16)
                sp.dma_start(w2[q][:], io["L0_ffn_W2"][e].rearrange("e (m p) n -> p (e m) n", p=P)).then_inc(w_loaded[q], 16)
                sp.dma_start(b2[q][:], io["L0_ffn_b2"][e].broadcast_to([P, D])).then_inc(w_loaded[q], 16)

            sp.dma_start(rows[0][:], rows_in[0]).then_inc(rows_loaded[0], 16)
            load_expert(Half(0), 0)
            sp.dma_start(rows[1][:], rows_in[1]).then_inc(rows_loaded[1], 16)
            load_expert(Half(2), 0)

            def do(st):
                if st.has(2, NH):
                    p = st.par(2)
                    wait_apart(sp, out_ready, st.n(1, 0, 1))
                    q = bass.ds(st.n(1, 2), 1)
                    sp.dma_start(rows[p][:].rearrange("p (q s) n -> p q s n", q=1),
                                 rows_in[q].rearrange("q p s n -> p q s n")).then_inc(rows_loaded[p], 16)
                if st.c % 2 == 1 and st.has(3, NH):
                    load_expert(st, 3)

            halves(sp, do, first=0)
            for p in range(2):
                wait_apart(sp, scattered[p], 16 * NS * NH // 2)

        @block.gpsimd
        def _(pool):
            nc.gpsimd.memset(ident[:], 0.0).then_inc(ident_zero, 1)
            wait_apart(pool, ident_zero, 1)
            nc.gpsimd.affine_select(out=ident[:], in_=ident[:], compare_op=ALU.not_equal, fill=1.0, base=0,
                                    pattern=[[-1, P]], channel_multiplier=1).then_inc(ident_ready, 1)

            def do(st):
                if st.has(1, NH):
                    p = st.par(1)
                    wait_apart(pool, rows_loaded[p], st.half(16, 1, 16))
                    if st.has(0, NH):
                        wait_apart(pool, xeT_done, st.n(2, 1))
                    for s in range(NS):
                        last = nc.gpsimd.tensor_scalar(xe[:, s, :], rows[p][:, s, 0:D], rows[p][:, s, D + 2:D + 3],
                                                       rows[p][:, s, D + 3:D + 4], ALU.subtract, ALU.mult)
                    last.then_inc(xe_ready, 1)
                if st.has(0, NH):
                    p = st.par(0)
                    wait_apart(pool, out_ready, st.n(1, 0, 1))
                    for s in range(NS):
                        nc.gpsimd.indirect_dma_start(
                            out=out2d, out_offset=bass.IndirectOffsetOnAxis(ap=ids[p][:, s:s + 1], axis=0),
                            in_=yo[p][:, s, :], in_offset=None, bounds_check=NT - 1, oob_is_err=False,
                        ).then_inc(scattered[p], 16)

            halves(pool, do)

        @block.scalar
        def _(act):
            def do(st):
                if st.has(0, NH):
                    p = st.par(0)
                    for m in range(MC):
                        act.wait_ge(h_done, st.n(MC, 0, m + 1))
                        if m == 0:
                            act.wait_ge(bias_ready, st.n(1, 0, 1))
                        if m == 0 and st.has(-2, NH):
                            act.wait_ge(y_done, st.n(NS, -1))
                        nc.scalar.activation(h[p][:, m, :], psH[m % 4][:], ACT.Relu, bias=bias[p][:, m:m + 1]).then_inc(h_kept, 1)

            halves(act, do, first=0)

        @block.vector
        def _(dve):
            dve.wait_ge(b1_turned, 1)
            nc.vector.tensor_copy(b1T[:], psT[0][:, 0:P]).then_inc(b1_kept, 1)
            dve.wait_ge(b1_kept, 1)

            def do(st):
                if st.has(1, NH):
                    p = st.par(1)
                    if st.has(-1, NH):
                        wait_apart(dve, h_kept, st.n(MC, 0))
                    nc.vector.tensor_copy(bias[p][:], b1T[:, bass.ds(st.expert(MC, 1), MC)]).then_inc(bias_ready, 1)
                    for c in range(DC):
                        dve.wait_ge(xeT_done, st.n(2, 1, c + 1))
                        if c == 0 and st.has(-1, NH):
                            dve.wait_ge(h_done, st.n(MC, 0))
                        nc.vector.tensor_copy(xeT[p][:, c, :], psT[c][:]).then_inc(xeT_kept, 1)
                if st.has(0, NH):
                    p = st.par(0)
                    if st.has(-2, NH):
                        dve.wait_ge(scattered[p], st.half(16 * NS, 0))
                    nc.vector.tensor_copy(ids[p][:], rows[p][:, :, D + 1])
                    for s in range(NS):
                        dve.wait_ge(y_done, st.n(NS, 0, s + 1))
                        nc.vector.tensor_tensor(y[s % 2][:], psY[s % 2][:, 0:D], b2[st.expar(0)][:], ALU.add).then_inc(y_kept, 1)
                        dve.wait_ge(y_kept, st.n(NS, 0, s + 1))
                        last = nc.vector.scalar_tensor_tensor(out=yo[p][:, s, :], in0=y[s % 2][:], scalar=rows[p][:, s, D:D + 1],
                                                              in1=rows[p][:, s, 0:D], op0=ALU.mult, op1=ALU.add)
                    last.then_inc(out_ready, 1)
                    dve.wait_ge(out_ready, st.n(1, 0, 1))

            halves(dve, do)

        @block.tensor
        def _(pe):
            pe.wait_ge(ident_ready, 1)
            pe.wait_ge(b1_loaded, 16)
            nc.tensor.transpose(psT[0][:, 0:P], b1in[:], ident[:]).then_inc(b1_turned, 1)
            pe.wait_ge(b1_kept, 1)

            def do(st):
                if st.has(0, NH):
                    p, q = st.par(0), st.expar(0)
                    pe.wait_ge(xeT_kept, st.n(2, 1))
                    pe.wait_ge(w_loaded[q], st.quarter(48, 0, 48))
                    for m in range(MC):
                        if m >= 4 or st.has(-1, NH):
                            pe.wait_ge(h_kept, st.n(MC, 0, m - 3))
                        for c in range(DC):
                            last = nc.tensor.matmul(psH[m % 4][:], w1[q][:, c, m * P:(m + 1) * P], xeT[p][:, c, :],
                                                    start=(c == 0), stop=(c == DC - 1))
                        last.then_inc(h_done, 1)
                if st.has(1, NH):
                    pe.wait_ge(xe_ready, st.n(1, 1, 1))
                    if st.has(0, NH):
                        pe.wait_ge(xeT_kept, st.n(2, 1))
                    for c in range(DC):
                        for s in range(NS):
                            last = nc.tensor.transpose(psT[c][:, s * P:(s + 1) * P], xe[:, s, c * P:(c + 1) * P], ident[:])
                        last.then_inc(xeT_done, 1)
                if st.has(0, NH):
                    for s in range(NS):
                        if s >= 2 or st.has(-1, NH):
                            pe.wait_ge(y_kept, st.n(NS, 0, s - 1))
                        for m in range(MC):
                            if s == 0:
                                pe.wait_ge(h_kept, st.n(MC, 0, m + 1))
                            last = nc.tensor.matmul(psY[s % 2][:, 0:D], h[p][:, m, s * P:(s + 1) * P], w2[q][:, m, :],
                                                    start=(m == 0), stop=(m == MC - 1))
                        last.then_inc(y_done, 1)

            halves(pe, do)


def build(nc, io):
    dr = {
        "rows": nc.dram_tensor("rows_dram", [NT, ROW], F32, kind="Internal").ap(),
        "qparts": nc.dram_tensor("qparts_dram", [2, 3, D, T], BF16, kind="Internal").ap(),
        "kparts": nc.dram_tensor("kparts_dram", [2, 3, D, T], BF16, kind="Internal").ap(),
        "maskrow": nc.dram_tensor("maskrow_dram", [B, S], BF16, kind="Internal").ap(),
    }
    with ExitStack() as ctx:
        def sem(name):
            return ctx.enter_context(nc.semaphore(name))

        attention_phase(nc, io, dr, sem)
        expert_phase(nc, io, dr, sem)


def kernel(**inputs):
    import numpy as _np
    import concourse.bacc as _bacc
    from concourse import mybir as _mybir
    from concourse.bass_utils import run_bass_kernel_spmd as _run

    nc = _bacc.Bacc("TRN2", target_bir_lowering=False, num_devices=1)
    arrays, io = {}, {}
    for name, value in inputs.items():
        a = _np.ascontiguousarray(value)
        if a.dtype == _np.bool_:
            a = a.view(_np.uint8)
        arrays[f"in_{name}"] = a
        io[name] = nc.dram_tensor(f"in_{name}", a.shape, _mybir.dt.from_np(a.dtype), kind="ExternalInput").ap()
    io["out"] = nc.dram_tensor("out_dram", (B, S, D), F32, kind="ExternalOutput").ap()
    build(nc, io)
    result = _run(nc, [arrays], core_ids=[0])
    return result.results[0]["out_dram"]
```

```python
from contextlib import ExitStack

import concourse.bass as bass
from concourse import mybir

F32 = mybir.dt.float32
F32R = mybir.dt.float32r
BF16 = mybir.dt.bfloat16
I32 = mybir.dt.int32
U8 = mybir.dt.uint8
ALU = mybir.AluOpType
ACT = mybir.ActivationFunctionType
AX_X = mybir.AxisListType.X

P = 128
B, S, D = 128, 128, 256
C = 192
CK = C // 2
H, HD = 16, 16
E, HID, CAP = 16, 1024, 1024
G = 4
NG = B // G
T = G * S
NT = B * S
DC = D // P
SCALE = float(HD) ** -0.5
EPS = 1e-5
BIG = 1e30
NOWHERE = float(4 * NT)
SLOTS = ((0, 0), (0, 1), (0, 2), (1, 0), (1, 1), (2, 0))
KROWS = len(SLOTS) * HD
VW = HD + 1
ROW = D + 4
MC = HID // P
NH = 2 * E
HS = CAP // 2


class Step:

    def __init__(self, c, j=None):
        self.c, self.j = c, j

    def has(self, d, n=NG):
        return self.j is not None or 0 <= self.c + d < n

    def n(self, per, d, k=0):
        const = per * (self.c + d) + k
        return const if self.j is None else self.j * (2 * per) + const

    def half(self, per, d, k=0):
        const = per * ((self.c + d) // 2) + k
        return const if self.j is None else self.j * per + const

    def par(self, d):
        return (self.c + d) % 2


def wait_apart(eng, sem, value):
    eng.wait_ge(sem, value)
    if not isinstance(value, int):
        eng.nop(nofuse=True)


def matmul_split(nc, out, a, b, first, last):
    nc.tensor.matmul(out, a[0], b[0], start=first, stop=False)
    nc.tensor.matmul(out, a[1], b[0], start=False, stop=False)
    return nc.tensor.matmul(out, a[0], b[1], start=False, stop=last)


class Chain:

    def __init__(self, eng, sem, per_loop=0):
        self.eng, self.sem, self.n, self.per_loop, self.j = eng, sem, 0, per_loop, None

    def mark(self, ins):
        ins.then_inc(self.sem, 1)
        self.n += 1
        return self.n

    def wait(self, n, apart=False):
        value = n if self.j is None else self.j * self.per_loop + n
        if apart:
            wait_apart(self.eng, self.sem, value)
        else:
            self.eng.wait_ge(self.sem, value)

    def link(self, ins, apart=False):
        self.wait(self.mark(ins), apart)

    def enter(self, j):
        self.j, self.n0 = j, self.n

    def leave(self, times):
        assert self.n - self.n0 == self.per_loop, (self.n - self.n0, self.per_loop)
        self.j, self.n = None, self.n0 + times * self.per_loop


def steps(eng, do, chain=None, first=-3, loop=(1, 13), last=NG):
    start, times = loop
    for c in range(first, start):
        do(Step(c))
    with eng.Fori(0, times) as j:
        if chain:
            chain.enter(j)
        do(Step(start, j))
        do(Step(start + 1, j))
        if chain:
            chain.leave(times)
    for c in range(start + 2 * times, last + 1):
        do(Step(c))


def attention_phase(nc, io, dr, sem):
    with ExitStack() as ctx:
        def sb(name, shape, dt=F32):
            return ctx.enter_context(nc.sbuf_tensor(name, shape, dt))

        def ps(name, shape, dt=F32):
            return ctx.enter_context(nc.psum_tensor(name, shape, dt))

        ident = sb("ident", [P, P])
        before = sb("before", [P, P], BF16)
        ones = sb("ones", [P, P], BF16)
        onesf = sb("onesf", [P, P])
        half_neg = sb("half_neg", [P, G])
        first_e = sb("first_e", [P, E])
        gate_bias = sb("gate_bias", [P, E])
        wq = sb("wq", [P, DC, D])
        wk = sb("wk", [CK, 2, D])
        wv = sb("wv", [CK, 2, D])
        wo = sb("wo", [P, DC, D])
        wg = sb("wg", [P, DC, P])
        maskrow = sb("maskrow", [B, S], BF16)
        anyrow = sb("anyrow", [B, 1])
        exp_scale = sb("exp_scale", [P, B])
        group_scale = [sb(f"group_scale{i}", [P, G]) for i in range(2)]
        empty_row = sb("empty_row", [P, ROW])
        x_in = [sb(f"x_in{i}", [P, G, D]) for i in range(2)]
        c_in = [sb(f"c_in{i}", [P, G, C]) for i in range(2)]
        xn = sb("xn", [P, G, D])
        xT = sb("xT", [P, DC, T])
        cT = [sb(f"cT{i}", [CK, 2, T]) for i in range(2)]
        parts = [sb(f"parts{i}", [P, DC, 3, T], BF16) for i in range(2)]
        rest = [sb(f"rest{i}", [P, T]) for i in range(2)]
        Qs = [sb(f"Qs{i}", [P, H, T], BF16) for i in range(2)]
        Ks = [sb(f"Ks{i}", [P, H, T], BF16) for i in range(2)]
        V = [sb(f"V{i}", [P, G, H * VW + 16]) for i in range(2)]
        M = sb("M", [P, G, H])
        Mparts = sb("Mparts", [H, 2, T], BF16)
        PT = [sb(f"PT{i}", [P, H, S]) for i in range(2)]
        OT = sb("OT", [P, G, S])
        On = sb("On", [P, H, HD])
        OnT = sb("OnT", [P, DC, S])
        inv = sb("inv", [P, H])
        xr = [sb(f"xr{i}", [P, G, ROW]) for i in range(2)]
        xn2 = sb("xn2", [P, G, D])
        x2T = sb("x2T", [P, DC, T])
        st1 = sb("st1", [P, G, 6])
        ag1 = sb("ag1", [P, G, 2])
        var1 = sb("var1", [P, G])
        var2 = sb("var2", [P, G])
        rstd1 = sb("rstd1", [P, G])
        st2 = sb("st2", [P, G, 6])
        ag2 = sb("ag2", [P, G, 2])
        lg = sb("lg", [P, G, E])
        lmax = sb("lmax", [P, G])
        hit = sb("hit", [P, G, E])
        best = sb("best", [P, G])
        onehot = sb("onehot", [P, G, E], BF16)
        expl = sb("expl", [P, G, E])
        count = sb("count", [P, E])
        seen = sb("seen", [P, E], BF16)
        seenf = sb("seenf", [P, E])
        posx = sb("posx", [P, G, E])
        pos = sb("pos", [P, G])
        over = sb("over", [P, G])
        slotf = sb("slotf", [P, G])
        esum = sb("esum", [P, G])
        sloti = [sb(f"sloti{i}", [P, G], I32) for i in range(2)]
        token = sb("token", [P, G])

        psA = [ps(f"psA{i}", [P, T]) for i in range(2)]
        psS1 = [ps(f"psS1{i}", [P, G, S]) for i in range(2)]
        psS2 = [ps(f"psS2{i}", [P, G, S]) for i in range(2)]
        psAV = ps("psAV", [P, G, S])
        psO = ps("psO", [P, T])

        def flat(bank):
            return bank[:].rearrange("p g s -> p (g s)")

        v_bank = (psA[1][:], flat(psS1[0]))
        xT_bank = (flat(psS1[1]), flat(psS2[0]))
        cT_bank = (flat(psS2[1]), psA[0][:])
        x2T_bank = (psA[1][:], flat(psS1[0]))
        qk_bank = (flat(psS2[0]), flat(psS1[1]), flat(psS2[1]), psA[0][:])

        x2d = io["x"].rearrange("b s d -> s b d")
        c2d = io["ctx_768"].rearrange("b s d -> s b d")
        out_sb = io["out"].rearrange("b s d -> s b d")

        weights_loaded = sem("weights_loaded")
        mask_loaded = sem("mask_loaded")
        maskrow_stored = sem("maskrow_stored")
        maskrow_ready = sem("maskrow_ready")
        rows_emptied = sem("rows_emptied")
        pool_const = sem("pool_const")
        pool_const2 = sem("pool_const2")
        dve_const = sem("dve_const")
        empty_ready = sem("empty_ready")
        any_ready = sem("any_ready")
        any_spread = sem("any_spread")
        x_loaded = [sem(f"x_loaded{i}") for i in range(2)]
        c_loaded = [sem(f"c_loaded{i}") for i in range(2)]
        xr_loaded = [sem(f"xr_loaded{i}") for i in range(2)]
        parts_stored = [sem(f"parts_stored{i}") for i in range(2)]
        stack_loaded = [sem(f"stack_loaded{i}") for i in range(2)]
        mrows_loaded = [sem(f"mrows_loaded{i}") for i in range(2)]
        x1_stored = [sem(f"x1_stored{i}") for i in range(2)]
        dispatched = [sem(f"dispatched{i}") for i in range(2)]
        mT_done, v_done, xT_done, cT_done, qk_done, x2T_done, lg_done, pos_done = (
            sem(x) for x in ("mT_done", "v_done", "xT_done", "cT_done", "qk_done", "x2T_done", "lg_done", "pos_done"))
        s1_done, s2_done, av_done, o_turned, on_turned, wo_done = (
            sem(x) for x in ("s1_done", "s2_done", "av_done", "o_turned", "on_turned", "wo_done"))
        v_kept, xT_kept, cT_kept, high_kept, middle_kept, x2T_kept, exp_done, ot_kept, onT_kept, expl_done = (
            sem(x) for x in ("v_kept", "xT_kept", "cT_kept", "high_kept", "middle_kept", "x2T_kept", "exp_done", "ot_kept",
                             "onT_kept", "expl_done"))
        xn_ready, xn2_ready, stats1, rest_ready, max_done, mparts_ready, norm_done, x1_done, stats2, lg_kept, oh_ready, route_ready, pos_kept = (
            sem(x) for x in ("xn_ready", "xn2_ready", "stats1", "rest_ready", "max_done", "mparts_ready", "norm_done", "x1_done", "stats2",
                             "lg_kept", "oh_ready", "route_ready", "pos_kept"))
        scale_ready = sem("scale_ready")
        dve_chain = sem("dve_chain")
        pool_chain = sem("pool_chain")
        low_ready, rstd1_ready, rstd2_ready = (sem(x) for x in ("low_ready", "rstd1_ready", "rstd2_ready"))

        block = ctx.enter_context(nc.Block())

        @block.sync
        def _(sp):
            sp.dma_start(x_in[0][:], x2d[:, 0:G, :]).then_inc(x_loaded[0], 16)
            sp.dma_start(c_in[0][:], c2d[:, 0:G, :]).then_inc(c_loaded[0], 16)
            sp.dma_start(xT[:, :, 0:D], io["L0_xattn_Wq"].rearrange("(c p) n -> p c n", p=P)).then_inc(weights_loaded, 16)
            sp.dma_start(cT[0][:, :, 0:D], io["L0_xattn_Wk"].rearrange("(c p) n -> p c n", p=CK)).then_inc(weights_loaded, 16)
            sp.dma_start(wv[:], io["L0_xattn_Wv"].rearrange("(c p) n -> p c n", p=CK)).then_inc(weights_loaded, 16)
            sp.dma_start(wo[:], io["L0_xattn_Wo"].rearrange("(c p) n -> p c n", p=P)).then_inc(weights_loaded, 16)
            sp.dma_start(gate_bias[:], io["L0_ffn_bg"].rearrange("(a n) -> a n", a=1).broadcast_to([P, E])).then_inc(weights_loaded, 16)
            sp.dma_start(lg[:, 0:DC, :], io["L0_ffn_Wg"].rearrange("(c p) n -> p c n", p=P)).then_inc(weights_loaded, 16)
            sp.dma_start(M[:, :, :].rearrange("p g h -> p (g h)").bitcast(U8)[:, 0:S], io["mask_BxS2_bf1"]).then_inc(mask_loaded, 16)
            wait_apart(sp, empty_ready, 1)
            rows = dr["rows"].rearrange("(p r) n -> p r n", p=P)
            sp.dma_start(rows, empty_row[:].rearrange("p (r n) -> p r n", r=1).broadcast_to([P, NT // P, ROW])).then_inc(rows_emptied, 16)
            wait_apart(sp, maskrow_ready, 1)
            sp.dma_start(dr["maskrow"], maskrow[:]).then_inc(maskrow_stored, 16)
            wait_apart(sp, maskrow_stored, 16)

            def step(st):
                if st.has(1):
                    p = st.par(1)
                    wait_apart(sp, parts_stored[p], st.half(64, 1, 64))
                    if st.has(-1):
                        wait_apart(sp, s2_done, st.n(4 * G, 0))
                    for i, (a, b) in enumerate(SLOTS):
                        sp.dma_start(Qs[p][i * HD:(i + 1) * HD, :, :],
                                     dr["qparts"][p, a].rearrange("(d h) t -> d h t", h=H)).then_inc(stack_loaded[p], 16)
                    for r0, n in ((0, 3), (3, 2), (5, 1)):
                        sp.dma_start(Ks[p][r0 * HD:(r0 + n) * HD, :, :],
                                     dr["kparts"][p, 0:n].rearrange("a (d h) t -> (a d) h t", h=H)).then_inc(stack_loaded[p], 16)
                    row = dr["maskrow"].rearrange("(g b) s -> g (b s)", b=G)[st.n(1, 1) if st.j is None else bass.ds(st.n(1, 1), 1)]
                    row = row.rearrange("(a t) -> a t", a=1) if st.j is None else row
                    sp.dma_start(Ks[p][KROWS:KROWS + 1, :, :],
                                 row.rearrange("a (h t) -> a h t", h=1).broadcast_to([1, H, T])).then_inc(stack_loaded[p], 16)
                if st.has(0):
                    p = st.par(0)
                    wait_apart(sp, mparts_ready, st.n(1, 0, 1))
                    for i in range(2):
                        sp.dma_start(Qs[p][KROWS + 1 + i:KROWS + 2 + i, :, :], Mparts[:, i, :]).then_inc(mrows_loaded[p], 16)
                if st.has(0):
                    p = st.par(0)
                    if st.has(-2):
                        wait_apart(sp, x1_stored[p], st.half(16, -2, 16))
                        wait_apart(sp, dispatched[p], st.half(16 * G, -2, 16 * G))
                    sp.dma_start(xr[p][:, :, 0:D], x2d[:, bass.ds(st.n(G, 0), G), :]).then_inc(xr_loaded[p], 16)
                if st.has(-1):
                    p = st.par(-1)
                    wait_apart(sp, x1_done, st.n(G, 0))
                    sp.dma_start(out_sb[:, bass.ds(st.n(G, -1), G), :], xr[p][:, :, 0:D]).then_inc(x1_stored[p], 16)
                if st.has(2):
                    p = st.par(2)
                    if st.has(0):
                        wait_apart(sp, stack_loaded[p], st.half(160, 0, 160))
                    for i in range(2 * DC):
                        name, c = ("qparts", "kparts")[i // DC], i % DC
                        wait_apart(sp, low_ready, st.n(2 * DC, 2, i + 1))
                        sp.dma_start(dr[name][p, :, c * P:(c + 1) * P, :].rearrange("a r t -> r a t"),
                                     parts[i // DC][:, c, :, :]).then_inc(parts_stored[p], 16)
                if st.has(4):
                    p = st.par(4)
                    if st.has(2):
                        wait_apart(sp, xn_ready, st.n(1, 2, 1))
                        wait_apart(sp, cT_done, st.n(2, 2, 2))
                    sp.dma_start(x_in[p][:], x2d[:, bass.ds(st.n(G, 4), G), :]).then_inc(x_loaded[p], 16)
                    sp.dma_start(c_in[p][:], c2d[:, bass.ds(st.n(G, 4), G), :]).then_inc(c_loaded[p], 16)

            steps(sp, step)
            for p in range(2):
                wait_apart(sp, x1_stored[p], 16 * NG // 2)
                wait_apart(sp, dispatched[p], 16 * G * NG // 2)

        @block.gpsimd
        def _(pool):
            nc.gpsimd.memset(ident[:], 0.0).then_inc(pool_const, 1)
            nc.gpsimd.memset(before[:], 0.0).then_inc(pool_const, 1)
            nc.gpsimd.memset(ones[:], 1.0).then_inc(pool_const, 1)
            nc.gpsimd.memset(onesf[:], 1.0).then_inc(pool_const, 1)
            nc.gpsimd.memset(half_neg[:], -0.5).then_inc(pool_const, 1)
            nc.gpsimd.iota(first_e[:], pattern=[[-1, E]], base=E, channel_multiplier=0,
                           allow_small_or_imprecise_dtypes=True).then_inc(pool_const, 1)
            nc.gpsimd.iota(token[:], pattern=[[S, G]], base=0, channel_multiplier=1,
                           allow_small_or_imprecise_dtypes=True).then_inc(pool_const, 1)
            wait_apart(pool, pool_const, 7)
            nc.gpsimd.affine_select(out=ident[:], in_=ident[:], compare_op=ALU.not_equal, fill=1.0, base=0,
                                    pattern=[[-1, P]], channel_multiplier=1).then_inc(pool_const2, 1)
            nc.gpsimd.affine_select(out=before[:], in_=before[:], compare_op=ALU.is_ge, fill=1.0, base=0,
                                    pattern=[[-1, P]], channel_multiplier=1).then_inc(pool_const2, 1)
            chain = Chain(pool, pool_chain, per_loop=4)

            def step(st):
                if st.has(-1):
                    p = st.par(-1)
                    wait_apart(pool, stats2, st.n(1, 0))
                    n = chain.mark(nc.gpsimd.tensor_scalar(var2[:], ag2[:, :, 1], EPS, None, ALU.add))
                    nc.gpsimd.tensor_copy(xr[p][:, :, D + 2], ag2[:, :, 0])
                    chain.wait(n, apart=True)
                    nc.gpsimd.tensor_tensor(xr[p][:, :, D + 3], var2[:], half_neg[:], ALU.pow).then_inc(rstd2_ready, 1)
                if st.has(2):
                    for i in range(2 * DC):
                        wait_apart(pool, middle_kept, st.n(2 * DC, 2, i + 1))
                        part, c = parts[i // DC], i % DC
                        nc.gpsimd.tensor_tensor(part[:, c, 2, :], rest[i % 2][:], part[:, c, 1, :],
                                                ALU.subtract).then_inc(low_ready, 1)
                if st.has(3):
                    wait_apart(pool, stats1, st.n(1, 4))
                    chain.link(nc.gpsimd.tensor_scalar(var1[:], ag1[:, :, 1], EPS, None, ALU.add), apart=True)
                    nc.gpsimd.tensor_tensor(rstd1[:], var1[:], half_neg[:], ALU.pow).then_inc(rstd1_ready, 1)
                if st.has(-1):
                    p = st.par(-1)
                    wait_apart(pool, rows_emptied, 16)
                    wait_apart(pool, route_ready, st.n(1, 0))
                    for b in range(G):
                        nc.gpsimd.indirect_dma_start(
                            out=dr["rows"], out_offset=bass.IndirectOffsetOnAxis(ap=sloti[p][:, b:b + 1], axis=0),
                            in_=xr[p][:, b, :], in_offset=None, bounds_check=NT - 1, oob_is_err=False,
                        ).then_inc(dispatched[p], 16)

            wait_apart(pool, pool_const2, 2)
            steps(pool, step, chain)

        @block.scalar
        def _(act):
            def on_turned_back(st, d, b):
                act.wait_ge(on_turned, st.n(G, d, b + 1))
                nc.scalar.copy(OnT[:].rearrange("p c s -> p (c s)"), psO[:, 0:D]).then_inc(onT_kept, 1)

            def high(st, i):
                act.wait_ge(qk_done, st.n(4, 2, i + 1))
                if i == 0 and st.has(1):
                    act.wait_ge(parts_stored[st.par(1)], st.half(64, 1, 64))
                nc.scalar.copy(parts[i // DC][:, i % DC, 0, :], qk_bank[i]).then_inc(high_kept, 1)

            def middle(st, i):
                act.wait_ge(rest_ready, st.n(4, 2, i + 1))
                nc.scalar.copy(parts[i // DC][:, i % DC, 1, :], rest[i % 2][:]).then_inc(middle_kept, 1)

            def step(st):
                if st.has(-1):
                    on_turned_back(st, -1, G - 2)
                if st.has(1):
                    p = st.par(1)
                    for i in range(2):
                        act.wait_ge(v_done, st.n(2, 1, i + 1))
                        if i == 0 and st.has(-1):
                            act.wait_ge(av_done, st.n(G, 0))
                        if i == 0:
                            act.wait_ge(dve_const, 1)
                        dst = V[p][:, 2 * i:2 * i + 2, 0:H * VW].rearrange("p b (h w) -> p b h w", w=VW)
                        for b in range(2):
                            last = nc.scalar.copy(dst[:, b, :, 0:HD], v_bank[i][:, b * D:(b + 1) * D].rearrange("p (h w) -> p h w", w=HD))
                        last.then_inc(v_kept, 1)
                if st.has(2):
                    for c in range(DC):
                        act.wait_ge(xT_done, st.n(2, 2, c + 1))
                        if c == 0:
                            act.wait_ge(dve_const, 1)
                            if st.has(1):
                                act.wait_ge(qk_done, st.n(4, 2))
                        nc.scalar.copy(xT[:, c, :], xT_bank[c]).then_inc(xT_kept, 1)
                if st.has(-1):
                    on_turned_back(st, -1, G - 1)
                if st.has(2):
                    p = st.par(2)
                    for c in range(2):
                        act.wait_ge(cT_done, st.n(2, 2, c + 1))
                        nc.scalar.copy(cT[p][:, c, :], cT_bank[c][0:CK, :]).then_inc(cT_kept, 1)
                    high(st, 0)
                    high(st, 1)
                    middle(st, 0)
                    high(st, 2)
                    middle(st, 1)
                if st.has(-1):
                    for c in range(DC):
                        act.wait_ge(x2T_done, st.n(2, -1, c + 1))
                        if c == 0 and st.has(-2):
                            act.wait_ge(lg_done, st.n(1, -1))
                        nc.scalar.copy(x2T[:, c, :], x2T_bank[c]).then_inc(x2T_kept, 1)
                if st.has(2):
                    middle(st, 2)
                    high(st, 3)
                for t in range(G + 1):
                    for k in range(4):
                        if st.has(0) and t < G:
                            act.wait_ge(s2_done, st.n(16, 0, 4 * t + k + 1))
                            if k == 0 and (t >= 2 or st.has(-1)):
                                act.wait_ge(av_done, st.n(G, 0, t - 1))
                            if t == 0 and k == 0:
                                act.wait_ge(scale_ready, st.n(1, 0, 1))
                            nc.scalar.activation(
                                PT[t % 2][:, 4 * k:4 * k + 4, :], psS2[k % 2][:], ACT.Exp,
                                scale=group_scale[st.par(0)][:, t:t + 1]).then_inc(exp_done, 1)
                        if t == 0 and k == 0 and st.has(2):
                            middle(st, 3)
                        if t == 1 and k == 1 and st.has(-1):
                            act.wait_ge(oh_ready, st.n(1, 0))
                            nc.scalar.activation(expl[:], lg[:], ACT.Exp).then_inc(expl_done, 1)
                        if k == 2 and 2 <= t < G and st.has(0):
                            on_turned_back(st, 0, t - 2)
                    if t >= 1 and st.has(0):
                        act.wait_ge(av_done, st.n(G, 0, t))
                        nc.scalar.copy(OT[:], psAV[:]).then_inc(ot_kept, 1)

            steps(act, step)

        @block.vector
        def _(dve):
            chain = Chain(dve, dve_chain)
            nc.vector.memset(empty_row[:], 0.0)
            chain.link(nc.vector.memset(seenf[:], 0.0))
            nc.vector.memset(empty_row[:, D + 1:D + 2], NOWHERE).then_inc(empty_ready, 1)
            nc.vector.memset(seen[:], 0.0)
            for p in range(2):
                nc.vector.memset(V[p][:], 1.0)
                nc.vector.memset(Qs[p][KROWS:KROWS + 3, :, :], 1.0)
                nc.vector.memset(Ks[p][KROWS:KROWS + 3, :, :], 1.0)
            nc.vector.memset(wg[:], 0.0)
            dve.wait_ge(mask_loaded, 16)
            mask8 = M[:, :, :].rearrange("p g h -> p (g h)").bitcast(U8)[:, 0:S]
            chain.link(nc.vector.tensor_copy(PT[0][:, 0, :], mask8))
            nc.vector.tensor_scalar(maskrow[:], PT[0][:, 0, :], 1.0, BIG, ALU.subtract, ALU.mult).then_inc(maskrow_ready, 1)
            chain.link(nc.vector.tensor_reduce(anyrow[:], PT[0][:, 0, :], AX_X, ALU.max))
            dve.wait_ge(pool_const2, 2)
            nc.vector.tensor_scalar(PT[0][:, 1, :], ident[:], anyrow[:, 0:1], SCALE, ALU.mult, ALU.mult).then_inc(any_ready, 1)
            dve.wait_ge(weights_loaded, 96)
            for c in range(DC):
                nc.vector.tensor_copy(wq[:, c, :].rearrange("p (d h) -> p d h", h=H),
                                      xT[:, c, 0:D].rearrange("p (h d) -> p d h", d=HD))
                nc.vector.tensor_copy(wk[:, c, :].rearrange("p (d h) -> p d h", h=H),
                                      cT[0][:, c, 0:D].rearrange("p (h d) -> p d h", d=HD))
            chain.link(nc.vector.tensor_copy(wg[:, :, 0:E], lg[:, 0:DC, :]))
            dve.sem_inc(dve_const, 1)
            dve.wait_ge(any_spread, 1)
            nc.vector.tensor_copy(exp_scale[:], psS2[0][:, 0, :]).then_inc(any_spread, 1)
            dve.wait_ge(any_spread, 2)

            def invert(st, d, b):
                dve.wait_ge(o_turned, st.n(G, d, b + 1))
                return chain.mark(nc.vector.reciprocal(inv[:], psO[:].rearrange("p (h w) -> p h w", w=32)[:, :, HD]))

            def norm(st, d, b, inverted):
                chain.wait(inverted)
                nc.vector.tensor_tensor(On[:], psO[:].rearrange("p (h w) -> p h w", w=32)[:, :, 0:HD],
                                        inv[:].rearrange("p (h w) -> p h w", w=1).broadcast_to([P, H, HD]),
                                        ALU.mult).then_inc(norm_done, 1)

            def add_residual(st, d, b):
                p = st.par(d)
                dve.wait_ge(wo_done, st.n(G, d, b + 1))
                if b == 0:
                    dve.wait_ge(xr_loaded[p], st.half(16, d, 16))
                nc.vector.tensor_tensor(xr[p][:, b, 0:D], psO[:, 0:D], xr[p][:, b, 0:D], ALU.add).then_inc(x1_done, 1)

            def stats_of_x1(st, d, b):
                dve.wait_ge(x1_done, st.n(G, d, b + 1))
                return chain.mark(nc.vector.bn_stats(st2[:, b, :], xr[st.par(d)][:, b, 0:D]))

            def maxima(st, t, k):
                if st.has(1) and t < G:
                    dve.wait_ge(s1_done, st.n(16, 1, 4 * t + k + 1))
                    if t == 0 and k == 0 and st.has(0):
                        dve.wait_ge(mT_done, st.n(1, 1))
                    nc.vector.tensor_reduce(M[:, t, 4 * k:4 * k + 4], psS1[k % 2][:], AX_X, ALU.max).then_inc(max_done, 1)

            def leave_rest(st, i):
                dve.wait_ge(high_kept, st.n(4, 2, i + 1))
                if i >= 2 or st.has(1):
                    dve.wait_ge(low_ready, st.n(4, 2, i - 1))
                nc.vector.tensor_tensor(rest[i % 2][:], qk_bank[i], parts[i // DC][:, i % DC, 0, :],
                                        ALU.subtract).then_inc(rest_ready, 1)

            def normalise(out, x, mean, rstd):
                return nc.vector.tensor_scalar(out, x, mean, rstd, ALU.subtract, ALU.mult)

            def spread(a):
                return a[:].rearrange("p (g e) -> p g e", e=1).broadcast_to([P, G, E])

            def step(st):
                p1, p3 = st.par(-1), st.par(3)
                route = st.has(-1)
                if st.has(0):
                    if st.has(-2):
                        wait_apart(dve, exp_done, st.n(16, -1))
                    nc.vector.tensor_copy(group_scale[st.par(0)][:], exp_scale[:, bass.ds(st.n(G, 0), G)]).then_inc(scale_ready, 1)
                    dve.wait_ge(mT_done, st.n(1, 0, 1))
                    if st.has(-1):
                        dve.wait_ge(mrows_loaded[st.par(-1)], st.half(32, -1, 32))
                    chain.link(nc.vector.tensor_scalar(Mparts[:, 0, :], psA[0][0:H, :], -1.0, None, ALU.mult))
                    nc.vector.scalar_tensor_tensor(out=Mparts[:, 1, :], in0=psA[0][0:H, :], scalar=-1.0,
                                                   in1=Mparts[:, 0, :], op0=ALU.mult, op1=ALU.subtract).then_inc(mparts_ready, 1)
                if st.has(-1):
                    add_residual(st, -1, G - 2)
                    stats_of_x1(st, -1, G - 2)
                    norm(st, -1, G - 1, invert(st, -1, G - 1))
                    add_residual(st, -1, G - 1)
                    chain.wait(stats_of_x1(st, -1, G - 1), apart=True)
                    for b in range(G):
                        last = nc.vector.bn_aggr(ag2[:, b, :], st2[:, b, :])
                    last.then_inc(stats2, 1)
                if st.has(2):
                    leave_rest(st, 0)
                if st.has(-1):
                    dve.wait_ge(rstd2_ready, st.n(1, 0))
                    if st.has(-2):
                        dve.wait_ge(x2T_done, st.n(2, -1))
                    for b in range(G):
                        last = normalise(xn2[:, b, :], xr[p1][:, b, 0:D], xr[p1][:, b, D + 2:D + 3], xr[p1][:, b, D + 3:D + 4])
                    last.then_inc(xn2_ready, 1)
                if st.has(2):
                    leave_rest(st, 1)
                    leave_rest(st, 2)
                    leave_rest(st, 3)

                if route:
                    dve.wait_ge(lg_done, st.n(1, 0))
                    nc.vector.tensor_tensor(lg[:], psA[1][:].rearrange("p (g e) -> p g e", e=P)[:, :, 0:E],
                                            gate_bias[:].rearrange("p (g e) -> p g e", g=1).broadcast_to([P, G, E]),
                                            ALU.add).then_inc(lg_kept, 1)
                maxima(st, 0, 0)
                if route:
                    dve.wait_ge(lg_kept, st.n(1, 0))
                    n = chain.mark(nc.vector.tensor_reduce(lmax[:], lg[:], AX_X, ALU.max))
                maxima(st, 0, 1)
                if route:
                    chain.wait(n)
                    n = chain.mark(nc.vector.tensor_tensor(hit[:], lg[:], spread(lmax), ALU.is_equal))
                maxima(st, 0, 2)
                if route:
                    chain.wait(n)
                    n = chain.mark(nc.vector.tensor_tensor(
                        hit[:], hit[:], first_e[:].rearrange("p (g e) -> p g e", g=1).broadcast_to([P, G, E]), ALU.mult))
                maxima(st, 0, 3)
                if route:
                    chain.wait(n)
                    n = chain.mark(nc.vector.tensor_reduce(best[:], hit[:], AX_X, ALU.max))

                def stats_of_x(t):
                    if st.has(3):
                        if t == 0:
                            dve.wait_ge(x_loaded[p3], st.half(16, 3, 16))
                        return chain.mark(nc.vector.bn_stats(st1[:, t, :], x_in[p3][:, t, :]))

                stats_of_x(0)

                maxima(st, 1, 0)
                if route:
                    chain.wait(n)
                    n = chain.mark(nc.vector.tensor_tensor(onehot[:], hit[:], spread(best), ALU.is_equal))
                    nc.vector.tensor_tensor(lg[:], lg[:], spread(lmax), ALU.subtract).then_inc(oh_ready, 1)
                maxima(st, 1, 1)
                if route:
                    chain.wait(n)
                    n = chain.mark(nc.vector.tensor_reduce(count[:], onehot[:].rearrange("p g e -> p e g"), AX_X, ALU.add))
                maxima(st, 1, 2)
                if route:
                    chain.wait(n)
                    counted = chain.mark(nc.vector.tensor_tensor(seenf[:], seenf[:], count[:], ALU.add))
                maxima(st, 1, 3)
                stats_of_x(1)

                maxima(st, 2, 0)
                if st.has(0):
                    n = invert(st, 0, 0)
                stats_of_x(2)
                if st.has(0):
                    norm(st, 0, 0, n)
                maxima(st, 2, 1)
                if route:
                    dve.wait_ge(pos_done, st.n(1, 0))
                    nc.vector.tensor_tensor(posx[:], psA[1][:, 0:G * E].rearrange("p (g e) -> p g e", e=E), onehot[:],
                                            ALU.mult).then_inc(pos_kept, 1)
                    chain.wait(counted)
                    nc.vector.tensor_copy(seen[:], seenf[:])
                maxima(st, 2, 2)
                if route:
                    dve.wait_ge(pos_kept, st.n(1, 0))
                    n = chain.mark(nc.vector.tensor_reduce(pos[:], posx[:], AX_X, ALU.add))
                    m = chain.mark(nc.vector.tensor_scalar(slotf[:], best[:], -float(CAP), float(CAP * E), ALU.mult, ALU.add))
                maxima(st, 2, 3)
                if route:
                    chain.wait(m)
                    nc.vector.tensor_scalar(over[:], pos[:], float(CAP), NOWHERE, ALU.is_ge, ALU.mult)
                    n = chain.mark(nc.vector.tensor_tensor(slotf[:], slotf[:], pos[:], ALU.add))

                if st.has(0):
                    add_residual(st, 0, 0)
                maxima(st, 3, 0)
                if st.has(0):
                    m = invert(st, 0, 1)
                all_stats = stats_of_x(3)
                if st.has(0):
                    norm(st, 0, 1, m)
                maxima(st, 3, 1)
                if st.has(3):
                    if st.j is None or st.has(3):
                        chain.wait(all_stats, apart=True)
                    for b in range(G):
                        last = nc.vector.bn_aggr(ag1[:, b, :], st1[:, b, :])
                    last.then_inc(stats1, 1)
                if st.has(0):
                    stats_of_x1(st, 0, 0)
                if route:
                    chain.wait(n)
                    nc.vector.tensor_tensor(sloti[p1][:], slotf[:], over[:], ALU.add)
                    dve.wait_ge(expl_done, st.n(1, 0))
                    n = chain.mark(nc.vector.tensor_reduce(esum[:], expl[:], AX_X, ALU.add))
                maxima(st, 3, 2)
                if route:
                    chain.wait(n)
                    nc.vector.reciprocal(xr[p1][:, :, D], esum[:])
                    nc.vector.tensor_copy(xr[p1][:, :, D + 1], token[:])
                    nc.vector.tensor_scalar(token[:], token[:], float(T), None, ALU.add).then_inc(route_ready, 1)
                maxima(st, 3, 3)

                if st.has(0):
                    add_residual(st, 0, 1)
                    norm(st, 0, 2, invert(st, 0, 2))
                if st.has(3):
                    dve.wait_ge(rstd1_ready, st.n(1, 4))
                    if st.has(2):
                        dve.wait_ge(xT_done, st.n(2, 3))
                    for b in range(G):
                        last = normalise(xn[:, b, :], x_in[p3][:, b, :], ag1[:, b, 0:1], rstd1[:, b:b + 1])
                    last.then_inc(xn_ready, 1)
                if st.has(0):
                    stats_of_x1(st, 0, 1)
                if route:
                    dve.wait_ge(route_ready, st.n(1, 0))
                if st.has(3):
                    dve.wait_ge(xn_ready, st.n(1, 4))

            chain.per_loop = 2 * (1 + 2 * G + G + 11)
            steps(dve, step, chain)

        @block.tensor
        def _(pe):
            pe.wait_ge(any_ready, 1)
            nc.tensor.matmul(psS2[0][:, 0, :], onesf[:], PT[0][:, 1, :], start=True, stop=True).then_inc(any_spread, 1)
            pe.wait_ge(dve_const, 1)
            pe.wait_ge(any_spread, 2)

            def turn_o(st, d, b):
                pe.wait_ge(ot_kept, st.n(G, d, b + 1))
                if b >= 1 or st.has(d - 1):
                    pe.wait_ge(x1_done, st.n(G, d, b))
                for g in range(4):
                    last = nc.tensor.transpose(psO[:, g * P:(g + 1) * P], OT[:, g, :], ident[:])
                last.then_inc(o_turned, 1)

            def turn_on(st, d, b):
                pe.wait_ge(norm_done, st.n(G, d, b + 1))
                for c in range(DC):
                    last = nc.tensor.transpose(psO[:, c * P:(c + 1) * P], On[:, c * 8:(c + 1) * 8, :].rearrange("p h w -> p (h w)"), ident[:])
                last.then_inc(on_turned, 1)

            def project(st, d, b):
                pe.wait_ge(onT_kept, st.n(G, d, b + 1))
                for c in range(DC):
                    last = nc.tensor.matmul(psO[:, 0:D], OnT[:, c, :], wo[:, c, :], start=(c == 0), stop=(c == DC - 1))
                last.then_inc(wo_done, 1)

            def queries_keys(st, i):
                w, a = ((wq, xT), (wk, cT[st.par(2)]))[i // DC]
                m = (i % DC) * P
                for c in range(2):
                    last = nc.tensor.matmul(qk_bank[i], w[:, c, m:m + P], a[:, c, :], start=(c == 0), stop=(c == 1))
                last.then_inc(qk_done, 1)

            def values(st, i):
                for b in range(2):
                    for c in range(2):
                        at = (2 * i + b) * S
                        last = nc.tensor.matmul(v_bank[i][:, b * D:(b + 1) * D], cT[st.par(1)][:, c, at:at + S], wv[:, c, :],
                                                start=(c == 0), stop=(c == 1))
                last.then_inc(v_done, 1)

            def turn(bank, src, cols, at, done):
                for b in range(G):
                    last = nc.tensor.transpose(bank[0:cols, b * P:(b + 1) * P], src[:, b, at:at + cols], ident[:])
                last.then_inc(done, 1)

            def between_scores(st):
                if st.has(1):
                    pe.wait_ge(rest_ready, st.n(4, 2))
                if st.has(0):
                    pe.wait_ge(max_done, st.n(16, 1))
                    for b in range(G):
                        last = nc.tensor.transpose(psA[0][0:H, b * P:(b + 1) * P], M[:, b, :], ident[:])
                    last.then_inc(mT_done, 1)
                if st.has(-1):
                    turn_on(st, -1, G - 2)
                if st.has(1):
                    if st.has(-2):
                        pe.wait_ge(pos_kept, st.n(1, -1))
                    values(st, 0)
                if st.has(-1):
                    project(st, -1, G - 2)
                if st.has(1):
                    values(st, 1)
                if st.has(-1):
                    turn_o(st, -1, G - 1)
                if st.has(2):
                    pe.wait_ge(xn_ready, st.n(1, 2, 1))
                    turn(xT_bank[0], xn, P, 0, xT_done)
                    if st.has(-1):
                        pe.wait_ge(exp_done, st.n(16, 0))
                    turn(xT_bank[1], xn, P, P, xT_done)
                if st.has(-1):
                    turn_on(st, -1, G - 1)
                if st.has(2):
                    p = st.par(2)
                    pe.wait_ge(c_loaded[p], st.half(16, 2, 16))
                    turn(cT_bank[0], c_in[p], CK, 0, cT_done)
                    if st.has(0):
                        pe.wait_ge(mparts_ready, st.n(1, 0, 1))
                    turn(cT_bank[1], c_in[p], CK, CK, cT_done)
                if st.has(-1):
                    project(st, -1, G - 1)
                if st.has(2):
                    pe.wait_ge(xT_kept, st.n(2, 2, 2))
                    queries_keys(st, 0)
                    queries_keys(st, 1)
                    pe.wait_ge(cT_kept, st.n(2, 2, 2))
                    queries_keys(st, 2)
                if st.has(-1):
                    pe.wait_ge(xn2_ready, st.n(1, 0))
                    if st.has(1):
                        pe.wait_ge(v_kept, st.n(2, 1, 2))
                    elif st.has(-2):
                        pe.wait_ge(pos_kept, st.n(1, -1))
                    turn(x2T_bank[0], xn2, P, 0, x2T_done)
                    turn(x2T_bank[1], xn2, P, P, x2T_done)
                if st.has(2):
                    queries_keys(st, 3)
                if st.has(-1):
                    pe.wait_ge(x2T_kept, st.n(2, 0))
                    for b in range(G):
                        for c in range(DC):
                            last = nc.tensor.matmul(psA[1][:, b * P:(b + 1) * P], x2T[:, c, b * P:(b + 1) * P], wg[:, c, :],
                                                    start=(c == 0), stop=(c == DC - 1))
                    last.then_inc(lg_done, 1)

            def positions(st):
                pe.wait_ge(oh_ready, st.n(1, 0))
                if st.has(-2):
                    pe.wait_ge(route_ready, st.n(1, -1))
                oh = onehot[:].rearrange("p g e -> p (g e)")
                nc.tensor.matmul(psA[1][:, 0:G * E], before[:], oh, start=True, stop=False)
                for b in range(G - 1):
                    for b2 in range(b + 1, G):
                        nc.tensor.matmul(psA[1][:, b2 * E:(b2 + 1) * E], ones[:], onehot[:, b, :], start=False, stop=False,
                                         skip_group_check=True)
                last = nc.tensor.matmul(psA[1][:, 0:G * E], ones[:],
                                        seen[:].rearrange("p (g e) -> p g e", g=1).broadcast_to([P, G, E]),
                                        start=False, stop=True)
                last.then_inc(pos_done, 1)

            def scores_by_key(st, t, k):
                if not st.has(0) or t == G:
                    return
                if t == 0 and k == 0:
                    pe.wait_ge(mrows_loaded[st.par(0)], st.half(32, 0, 32))
                if t == 0 and k < 2 and st.has(2):
                    pe.wait_ge(rest_ready, st.n(4, 2, 1 + 2 * k))
                elif t or k >= 2 or st.has(-1):
                    pe.wait_ge(exp_done, st.n(16, 0, 4 * t + k - 1))
                p, r = st.par(0), KROWS + 3
                for i in range(4):
                    h = 4 * k + i
                    last = nc.tensor.matmul(psS2[k % 2][:, i, :], Ks[p][0:r, h, t * S:(t + 1) * S],
                                            Qs[p][0:r, h, t * S:(t + 1) * S], start=True, stop=True)
                last.then_inc(s2_done, 1)

            def scores_by_query(st, t, k):
                if not st.has(1) or t == G:
                    return
                if t == 0 and k == 0:
                    pe.wait_ge(stack_loaded[st.par(1)], st.half(160, 1, 160))
                    if st.has(-1):
                        pe.wait_ge(x2T_kept, st.n(2, 0))
                    else:
                        pe.wait_ge(v_kept, st.n(2, 1, 2))
                elif t == 0 and k == 1 and st.has(2):
                    pe.wait_ge(rest_ready, st.n(4, 2, 2))
                elif t or k >= 2:
                    pe.wait_ge(max_done, st.n(16, 1, 4 * t + k - 1))
                p, r = st.par(1), KROWS + 1
                for i in range(4):
                    h = 4 * k + i
                    last = nc.tensor.matmul(psS1[k % 2][:, i, :], Qs[p][0:r, h, t * S:(t + 1) * S],
                                            Ks[p][0:r, h, t * S:(t + 1) * S], start=True, stop=True)
                last.then_inc(s1_done, 1)

            def weigh_values(st, t, k):
                if not st.has(0) or t == 0:
                    return
                pe.wait_ge(exp_done, st.n(16, 0, 4 * (t - 1) + k + 1))
                if t == 1 and k == 0:
                    pe.wait_ge(v_kept, st.n(2, 1))
                if k == 0 and (t >= 2 or st.has(-1)):
                    pe.wait_ge(ot_kept, st.n(G, 0, t - 1))
                for i in range(4):
                    h = 4 * k + i
                    last = nc.tensor.matmul(psAV[32 * i:32 * i + 32, k, :], V[st.par(0)][:, t - 1, h * VW:h * VW + 32],
                                            PT[(t - 1) % 2][:, h, :], start=True, stop=True)
                if k == 3:
                    last.then_inc(av_done, 1)

            def step(st):
                between_scores(st)
                for t in range(G + 1):
                    result = st.has(0) and t >= 2
                    scores_by_key(st, t, 0)
                    scores_by_query(st, t, 0)
                    weigh_values(st, t, 0)
                    if result:
                        turn_o(st, 0, t - 2)
                    if t == 2 and st.has(-1):
                        positions(st)
                    scores_by_key(st, t, 1)
                    weigh_values(st, t, 1)
                    scores_by_query(st, t, 1)
                    scores_by_key(st, t, 2)
                    weigh_values(st, t, 2)
                    if result and t < G:
                        turn_on(st, 0, t - 2)
                    scores_by_query(st, t, 2)
                    scores_by_key(st, t, 3)
                    weigh_values(st, t, 3)
                    scores_by_query(st, t, 3)
                    if result and t < G:
                        project(st, 0, t - 2)

            steps(pe, step)


def expert_phase(nc, io, dr, sem):
    with ExitStack() as ctx:
        def sb(name, shape, dt=F32):
            return ctx.enter_context(nc.sbuf_tensor(name, shape, dt))

        def ps(name, shape, dt=F32):
            return ctx.enter_context(nc.psum_tensor(name, shape, dt))

        NS = HS // P
        ident = sb("ident2", [P, P])
        b1in = sb("b1in", [P, P])
        b1T = sb("b1T", [P, E * MC])
        bias = [sb(f"bias{i}", [P, MC]) for i in range(2)]
        w1_in = sb("w1_in", [P, DC, HID])
        w2_in = sb("w2_in", [P, MC, D])
        w1 = [[sb(f"w1_{n}{i}", [P, DC, HID], F32R) for n in ("high", "low")] for i in range(2)]
        w2 = [[sb(f"w2_{n}{i}", [P, MC, D], F32R) for n in ("high", "low")] for i in range(2)]
        b2 = [sb(f"b2_{i}", [P, D]) for i in range(2)]
        rows = [sb(f"rows{i}", [P, NS, ROW]) for i in range(2)]
        ids = [sb(f"ids{i}", [P, NS], I32) for i in range(2)]
        xe = sb("xe", [P, NS, D])
        xeT = [[sb(f"xeT_{n}{i}", [P, DC, HS], F32R) for n in ("high", "low")] for i in range(2)]
        hf = [sb(f"hf{i}", [P, HS]) for i in range(2)]
        h = [sb(f"h_{n}", [P, MC, HS], F32R) for n in ("high", "low")]
        y = [sb(f"y{i}", [P, D]) for i in range(2)]
        yo = [sb(f"yo{i}", [P, NS, D]) for i in range(2)]
        psT = [ps(f"psT{i}", [P, HS]) for i in range(2)]
        psH = [ps(f"psH{i}", [P, HS]) for i in range(4)]
        psY = [ps(f"psY{i}", [P, HS]) for i in range(2)]

        ident_zero, ident_ready, b1_loaded, b1_turned, b1_kept = (
            sem(x) for x in ("ident_zero", "ident_ready", "b1_loaded", "b1_turned", "b1_kept"))
        rows_loaded = [sem(f"rows_loaded{i}") for i in range(2)]
        w_loaded = sem("w_loaded")
        b2_loaded = [sem(f"b2_loaded{i}") for i in range(2)]
        w_high_ready, w_ready = sem("w_high_ready"), sem("w_ready")
        scattered = [sem(f"scattered{i}") for i in range(2)]
        bias_ready = sem("bias_ready")
        xe_ready, xeT_done, xeT_high_ready, xeT_ready, h_done, hf_kept, h_high_ready, h_ready = (
            sem(x) for x in ("xe_ready", "xeT_done", "xeT_high_ready", "xeT_ready", "h_done", "hf_kept",
                             "h_high_ready", "h_ready"))
        y_done, y_kept, out_ready = (sem(x) for x in ("y_done", "y_kept", "out_ready"))
        rows_in = dr["rows"].rearrange("(q s p) n -> q p s n", p=P, s=NS)
        out2d = io["out"].rearrange("b s d -> (b s) d")

        class Half(Step):

            def n(self, per, d, k=0):
                const = per * (self.c + d) + k
                return const if self.j is None else self.j * (4 * per) + const

            def half(self, per, d, k=0):
                const = per * ((self.c + d) // 2) + k
                return const if self.j is None else self.j * (2 * per) + const

            def expert(self, per, d, k=0):
                return self.half(per, d, k)

            def quarter(self, per, d, k=0):
                const = per * ((self.c + d) // 4) + k
                return const if self.j is None else self.j * per + const

            def expar(self, d):
                return (self.c + d) // 2 % 2

        def halves(eng, do, first=-1):
            for c in range(first, 4):
                do(Half(c))
            with eng.Fori(0, NH // 4 - 2) as j:
                for c in range(4):
                    do(Half(4 + c, j))
            for c in range(NH - 4, NH):
                do(Half(c))

        block = ctx.enter_context(nc.Block())

        @block.sync
        def _(sp):
            sp.dma_start(b1in[:], io["L0_ffn_b1"].rearrange("e (m p) -> (e m) p", p=P)).then_inc(b1_loaded, 16)

            def load_expert(st, d):
                q = st.expar(d)
                e = bass.ds(st.expert(1, d), 1)
                sp.dma_start(w1_in[:], io["L0_ffn_W1"][e].rearrange("e (c p) n -> p (e c) n", p=P)).then_inc(w_loaded, 16)
                sp.dma_start(w2_in[:], io["L0_ffn_W2"][e].rearrange("e (m p) n -> p (e m) n", p=P)).then_inc(w_loaded, 16)
                sp.dma_start(b2[q][:], io["L0_ffn_b2"][e].broadcast_to([P, D])).then_inc(b2_loaded[q], 16)

            sp.dma_start(rows[0][:], rows_in[0]).then_inc(rows_loaded[0], 16)
            load_expert(Half(0), 0)
            sp.dma_start(rows[1][:], rows_in[1]).then_inc(rows_loaded[1], 16)
            wait_apart(sp, w_ready, 1)
            load_expert(Half(2), 0)

            def do(st):
                if st.has(2, NH):
                    p = st.par(2)
                    wait_apart(sp, out_ready, st.n(1, 0, 1))
                    q = bass.ds(st.n(1, 2), 1)
                    sp.dma_start(rows[p][:].rearrange("p (q s) n -> p q s n", q=1),
                                 rows_in[q].rearrange("q p s n -> p q s n")).then_inc(rows_loaded[p], 16)
                if st.c % 2 == 1 and st.has(3, NH):
                    wait_apart(sp, w_ready, st.expert(1, 3))
                    load_expert(st, 3)

            halves(sp, do, first=0)
            for p in range(2):
                wait_apart(sp, scattered[p], 16 * NS * NH // 2)

        @block.gpsimd
        def _(pool):
            nc.gpsimd.memset(ident[:], 0.0).then_inc(ident_zero, 1)
            wait_apart(pool, ident_zero, 1)
            nc.gpsimd.affine_select(out=ident[:], in_=ident[:], compare_op=ALU.not_equal, fill=1.0, base=0,
                                    pattern=[[-1, P]], channel_multiplier=1).then_inc(ident_ready, 1)

            def do(st):
                if st.has(1, NH):
                    p = st.par(1)
                    wait_apart(pool, rows_loaded[p], st.half(16, 1, 16))
                    if st.has(0, NH):
                        wait_apart(pool, xeT_done, st.n(2, 1))
                    for s in range(NS):
                        last = nc.gpsimd.tensor_scalar(xe[:, s, :], rows[p][:, s, 0:D], rows[p][:, s, D + 2:D + 3],
                                                       rows[p][:, s, D + 3:D + 4], ALU.subtract, ALU.mult)
                    last.then_inc(xe_ready, 1)
                if st.has(0, NH):
                    p = st.par(0)
                    wait_apart(pool, out_ready, st.n(1, 0, 1))
                    for s in range(NS):
                        nc.gpsimd.indirect_dma_start(
                            out=out2d, out_offset=bass.IndirectOffsetOnAxis(ap=ids[p][:, s:s + 1], axis=0),
                            in_=yo[p][:, s, :], in_offset=None, bounds_check=NT - 1, oob_is_err=False,
                        ).then_inc(scattered[p], 16)

            halves(pool, do)

        @block.scalar
        def _(act):
            def high_of_xe(st, d):
                p = st.par(d)
                for c in range(DC):
                    act.wait_ge(xeT_done, st.n(2, d, c + 1))
                    if c == 0 and st.has(d - 2, NH):
                        act.wait_ge(h_done, st.n(MC, d - 1))
                    nc.scalar.copy(xeT[p][0][:, c, :], psT[c][:]).then_inc(xeT_high_ready, 1)

            def high_of_weights(st, d):
                q = st.expar(d)
                act.wait_ge(w_loaded, st.expert(32, d, 32))
                if st.has(d - 4, NH):
                    act.wait_ge(y_done, st.n(NS, d - 2))
                for c in range(DC):
                    nc.scalar.copy(w1[q][0][:, c, :], w1_in[:, c, :]).then_inc(w_high_ready, 1)
                for c in range(2):
                    m = slice(c * MC // 2, (c + 1) * MC // 2)
                    nc.scalar.copy(w2[q][0][:, m, :], w2_in[:, m, :]).then_inc(w_high_ready, 1)

            def hidden(st, m):
                p = st.par(0)
                act.wait_ge(h_done, st.n(MC, 0, m + 1))
                if m == 0:
                    act.wait_ge(bias_ready, st.n(1, 0, 1))
                if m >= 2 or st.has(-1, NH):
                    act.wait_ge(h_ready, st.n(MC, 0, m - 1))
                nc.scalar.activation(hf[m % 2][:], psH[m % 4][:], ACT.Relu, bias=bias[p][:, m:m + 1]).then_inc(hf_kept, 1)
                if m == 0 and st.has(-1, NH):
                    act.wait_ge(y_done, st.n(NS, 0))
                nc.scalar.activation(h[0][:, m, :], psH[m % 4][:], ACT.Relu, bias=bias[p][:, m:m + 1]).then_inc(h_high_ready, 1)

            high_of_weights(Half(0), 0)

            def do(st):
                if st.has(0, NH):
                    for m in range(MC):
                        hidden(st, m)
                if st.has(1, NH):
                    high_of_xe(st, 1)
                if st.c % 2 == 0 and st.has(2, NH):
                    high_of_weights(st, 2)

            halves(act, do)

        @block.vector
        def _(dve):
            dve.wait_ge(b1_turned, 1)
            nc.vector.tensor_copy(b1T[:], psT[0][:, 0:P]).then_inc(b1_kept, 1)
            dve.wait_ge(b1_kept, 1)

            def low(part, whole, high):
                return nc.vector.tensor_tensor(part, whole, high.bitcast(F32), ALU.subtract)

            def low_of_weights(st, d, i):
                q, c = st.expar(d), i % 2
                dve.wait_ge(w_high_ready, st.expert(4, d, i + 1))
                if i == 0 and st.has(d - 4, NH):
                    dve.wait_ge(y_done, st.n(NS, d - 2))
                if i < 2:
                    last = low(w1[q][1][:, c, :], w1_in[:, c, :], w1[q][0][:, c, :])
                else:
                    m = slice(c * MC // 2, (c + 1) * MC // 2)
                    last = low(w2[q][1][:, m, :], w2_in[:, m, :], w2[q][0][:, m, :])
                if i == 3:
                    last.then_inc(w_ready, 1)

            def low_of_xe(st, d):
                p = st.par(d)
                for c in range(DC):
                    dve.wait_ge(xeT_high_ready, st.n(2, d, c + 1))
                    low(xeT[p][1][:, c, :], psT[c][:], xeT[p][0][:, c, :]).then_inc(xeT_ready, 1)

            for i in range(4):
                low_of_weights(Half(0), 0, i)

            def do(st):
                if st.has(1, NH):
                    p = st.par(1)
                    if st.has(-1, NH):
                        wait_apart(dve, h_high_ready, st.n(MC, 0))
                    nc.vector.tensor_copy(bias[p][:], b1T[:, bass.ds(st.expert(MC, 1), MC)]).then_inc(bias_ready, 1)
                if st.has(0, NH):
                    for m in range(MC):
                        dve.wait_ge(h_high_ready, st.n(MC, 0, m + 1))
                        low(h[1][:, m, :], hf[m % 2][:], h[0][:, m, :]).then_inc(h_ready, 1)
                if st.has(1, NH):
                    low_of_xe(st, 1)
                if st.has(0, NH):
                    p = st.par(0)
                    if st.has(-2, NH):
                        dve.wait_ge(scattered[p], st.half(16 * NS, 0))
                    nc.vector.tensor_copy(ids[p][:], rows[p][:, :, D + 1])
                    dve.wait_ge(b2_loaded[st.expar(0)], st.quarter(16, 0, 16))
                    for s in range(NS):
                        dve.wait_ge(y_done, st.n(NS, 0, s + 1))
                        nc.vector.tensor_tensor(y[s % 2][:], psY[s % 2][:, 0:D], b2[st.expar(0)][:], ALU.add).then_inc(y_kept, 1)
                        if st.c % 2 == 0 and st.has(2, NH):
                            low_of_weights(st, 2, s)
                        dve.wait_ge(y_kept, st.n(NS, 0, s + 1))
                        last = nc.vector.scalar_tensor_tensor(out=yo[p][:, s, :], in0=y[s % 2][:], scalar=rows[p][:, s, D:D + 1],
                                                              in1=rows[p][:, s, 0:D], op0=ALU.mult, op1=ALU.add)
                    last.then_inc(out_ready, 1)
                    dve.wait_ge(out_ready, st.n(1, 0, 1))

            halves(dve, do)

        @block.tensor
        def _(pe):
            pe.wait_ge(ident_ready, 1)
            pe.wait_ge(b1_loaded, 16)
            nc.tensor.transpose(psT[0][:, 0:P], b1in[:], ident[:]).then_inc(b1_turned, 1)
            pe.wait_ge(b1_kept, 1)

            def do(st):
                if st.has(0, NH):
                    p, q = st.par(0), st.expar(0)
                    pe.wait_ge(xeT_ready, st.n(2, 1))
                    pe.wait_ge(w_ready, st.expert(1, 0, 1))
                    for m in range(MC):
                        if m >= 4 or st.has(-1, NH):
                            pe.wait_ge(h_high_ready, st.n(MC, 0, m - 3))
                        for c in range(DC):
                            last = matmul_split(nc, psH[m % 4][:], [w[:, c, m * P:(m + 1) * P] for w in w1[q]],
                                                [a[:, c, :] for a in xeT[p]], c == 0, c == DC - 1)
                        last.then_inc(h_done, 1)
                if st.has(1, NH):
                    pe.wait_ge(xe_ready, st.n(1, 1, 1))
                    if st.has(0, NH):
                        pe.wait_ge(xeT_ready, st.n(2, 1))
                    for c in range(DC):
                        for s in range(NS):
                            last = nc.tensor.transpose(psT[c][:, s * P:(s + 1) * P], xe[:, s, c * P:(c + 1) * P], ident[:])
                        last.then_inc(xeT_done, 1)
                if st.has(0, NH):
                    for s in range(NS):
                        if s >= 2 or st.has(-1, NH):
                            pe.wait_ge(y_kept, st.n(NS, 0, s - 1))
                        for m in range(MC):
                            if s == 0:
                                pe.wait_ge(h_ready, st.n(MC, 0, m + 1))
                            last = matmul_split(nc, psY[s % 2][:, 0:D], [a[:, m, s * P:(s + 1) * P] for a in h],
                                                [w[:, m, :] for w in w2[q]], m == 0, m == MC - 1)
                        last.then_inc(y_done, 1)

            halves(pe, do)


def build(nc, io):
    dr = {
        "rows": nc.dram_tensor("rows_dram", [NT, ROW], F32, kind="Internal").ap(),
        "qparts": nc.dram_tensor("qparts_dram", [2, 3, D, T], BF16, kind="Internal").ap(),
        "kparts": nc.dram_tensor("kparts_dram", [2, 3, D, T], BF16, kind="Internal").ap(),
        "maskrow": nc.dram_tensor("maskrow_dram", [B, S], BF16, kind="Internal").ap(),
    }
    with ExitStack() as ctx:
        def sem(name):
            return ctx.enter_context(nc.semaphore(name))

        attention_phase(nc, io, dr, sem)
        expert_phase(nc, io, dr, sem)


def kernel(**inputs):
    import numpy as _np
    import concourse.bacc as _bacc
    from concourse import mybir as _mybir
    from concourse.bass_utils import run_bass_kernel_spmd as _run

    nc = _bacc.Bacc("TRN2", target_bir_lowering=False, num_devices=1)
    arrays, io = {}, {}
    for name, value in inputs.items():
        a = _np.ascontiguousarray(value)
        if a.dtype == _np.bool_:
            a = a.view(_np.uint8)
        arrays[f"in_{name}"] = a
        io[name] = nc.dram_tensor(f"in_{name}", a.shape, _mybir.dt.from_np(a.dtype), kind="ExternalInput").ap()
    io["out"] = nc.dram_tensor("out_dram", (B, S, D), F32, kind="ExternalOutput").ap()
    build(nc, io)
    result = _run(nc, [arrays], core_ids=[0])
    return result.results[0]["out_dram"]
```

```python
from contextlib import ExitStack

import concourse.bass as bass
from concourse import mybir

F32 = mybir.dt.float32
F32R = mybir.dt.float32r
BF16 = mybir.dt.bfloat16
I32 = mybir.dt.int32
U8 = mybir.dt.uint8
ALU = mybir.AluOpType
ACT = mybir.ActivationFunctionType
AX_X = mybir.AxisListType.X

P = 128
B, S, D = 128, 128, 256
C = 192
CK = C // 2
H, HD = 16, 16
E, HID, CAP = 16, 1024, 1024
G = 4
NG = B // G
T = G * S
NT = B * S
DC = D // P
SCALE = float(HD) ** -0.5
EPS = 1e-5
BIG = 1e30
TWO_ONES = 1 + 2.0 ** -9 - 2.0 ** -16
EMPTYING = 16
NOWHERE = float(4 * NT)
SLOTS = ((0, 0), (0, 1), (0, 2), (1, 0), (1, 1), (2, 0))
KROWS = len(SLOTS) * HD
VW = HD + 1
ROW = D + 4
MC = HID // P
NH = 2 * E
HS = CAP // 2


class Step:

    def __init__(self, c, j=None):
        self.c, self.j = c, j

    def has(self, d, n=NG):
        return self.j is not None or 0 <= self.c + d < n

    def n(self, per, d, k=0):
        const = per * (self.c + d) + k
        return const if self.j is None else self.j * (2 * per) + const

    def half(self, per, d, k=0):
        const = per * ((self.c + d) // 2) + k
        return const if self.j is None else self.j * per + const

    def par(self, d):
        return (self.c + d) % 2


def wait_apart(eng, sem, value):
    eng.wait_ge(sem, value)
    if not isinstance(value, int):
        eng.nop(nofuse=True)


def matmul_split(nc, out, a, b, first, last):
    nc.tensor.matmul(out, a[0], b[0], start=first, stop=False)
    nc.tensor.matmul(out, a[1], b[0], start=False, stop=False)
    return nc.tensor.matmul(out, a[0], b[1], start=False, stop=last)


class Chain:

    def __init__(self, eng, sem, per_loop=0):
        self.eng, self.sem, self.n, self.per_loop, self.j = eng, sem, 0, per_loop, None

    def mark(self, ins):
        ins.then_inc(self.sem, 1)
        self.n += 1
        return self.n

    def wait(self, n, apart=False):
        value = n if self.j is None else self.j * self.per_loop + n
        if apart:
            wait_apart(self.eng, self.sem, value)
        else:
            self.eng.wait_ge(self.sem, value)

    def link(self, ins, apart=False):
        self.wait(self.mark(ins), apart)

    def enter(self, j):
        self.j, self.n0 = j, self.n

    def leave(self, times):
        assert self.n - self.n0 == self.per_loop, (self.n - self.n0, self.per_loop)
        self.j, self.n = None, self.n0 + times * self.per_loop


def steps(eng, do, chain=None, first=-3, loop=(1, 13), last=NG):
    start, times = loop
    for c in range(first, start):
        do(Step(c))
    with eng.Fori(0, times) as j:
        if chain:
            chain.enter(j)
        do(Step(start, j))
        do(Step(start + 1, j))
        if chain:
            chain.leave(times)
    for c in range(start + 2 * times, last + 1):
        do(Step(c))


def attention_phase(nc, io, dr, sem, both):
    with ExitStack() as ctx:
        def sb(name, shape, dt=F32):
            return ctx.enter_context(nc.sbuf_tensor(name, shape, dt))

        def ps(name, shape, dt=F32):
            return ctx.enter_context(nc.psum_tensor(name, shape, dt))

        ident = both["ident"]
        before = sb("before", [P, P], BF16)
        ones = sb("ones", [P, P], BF16)
        onesf = sb("onesf", [P, P])
        half_neg = sb("half_neg", [P, G])
        first_e = sb("first_e", [P, E])
        gate_bias = sb("gate_bias", [P, E])
        wq = [sb(f"wq_{n}", [P, DC, D], F32R) for n in ("high", "low")]
        wk = [sb(f"wk_{n}", [CK, 2, D], F32R) for n in ("high", "low")]
        wv = [sb(f"wv_{n}", [CK, 2, D], F32R) for n in ("high", "low")]
        wo = [sb(f"wo_{n}", [P, DC, D], F32R) for n in ("high", "low")]
        wg = sb("wg", [P, DC, P])
        maskrow = sb("maskrow", [B, S], BF16)
        anyrow = sb("anyrow", [B, 1])
        exp_scale = sb("exp_scale", [P, B])
        group_scale = [sb(f"group_scale{i}", [P, G]) for i in range(2)]
        empty_row = sb("empty_row", [P, ROW])
        x_in = [both["wide"][:, i, :].rearrange("p (g n) -> p g n", g=G) for i in range(2)]
        c_in = [sb(f"c_in{i}", [P, G, C]) for i in range(2)]
        xn = sb("xn", [P, G, D])
        xT = [sb(f"xT_{n}", [P, DC, T], F32R) for n in ("high", "low")]
        cT = [[sb(f"cT_{n}{i}", [CK, 2, T], F32R) for n in ("high", "low")] for i in range(2)]
        parts = [sb(f"parts{i}", [P, DC, 3, T], BF16) for i in range(2)]
        rest = [both["deep"][:, i, :] for i in range(2 * DC)]
        Qs = [sb(f"Qs{i}", [P, H, T], BF16) for i in range(2)]
        Ks = [sb(f"Ks{i}", [P, H, T], BF16) for i in range(2)]
        V = [sb(f"V{i}", [P, G, H * VW + 16]) for i in range(2)]
        M = sb("M", [P, G, H])
        Mparts = sb("Mparts", [H, 2, T], BF16)
        PT = [sb(f"PT{i}", [P, H, S]) for i in range(2)]
        OT = sb("OT", [P, G, S])
        On = sb("On", [P, H, HD])
        OnT = [sb(f"OnT_{n}", [P, DC, S], F32R) for n in ("high", "low")]
        inv = sb("inv", [P, H])
        xr = [sb(f"xr{i}", [P, G, ROW]) for i in range(2)]
        xn2 = sb("xn2", [P, G, D])
        x2T = sb("x2T", [P, DC, T])
        st1 = sb("st1", [P, G, 6])
        ag1 = sb("ag1", [P, G, 2])
        var1 = sb("var1", [P, G])
        var2 = sb("var2", [P, G])
        rstd1 = sb("rstd1", [P, G])
        st2 = sb("st2", [P, G, 6])
        ag2 = sb("ag2", [P, G, 2])
        lg = sb("lg", [P, G, E])
        lmax = sb("lmax", [P, G])
        hit = sb("hit", [P, G, E])
        best = sb("best", [P, G])
        onehot = sb("onehot", [P, G, E], BF16)
        expl = sb("expl", [P, G, E])
        count = sb("count", [P, E])
        seen = sb("seen", [P, E], BF16)
        seenf = sb("seenf", [P, E])
        posx = sb("posx", [P, G, E])
        pos = sb("pos", [P, G])
        over = sb("over", [P, G])
        slotf = sb("slotf", [P, G])
        esum = sb("esum", [P, G])
        sloti = [sb(f"sloti{i}", [P, G], I32) for i in range(2)]
        token = sb("token", [P, G])

        psA = [ps(f"psA{i}", [P, T]) for i in range(2)]
        psS1 = [ps(f"psS1{i}", [P, G, S]) for i in range(2)]
        psS2 = [ps(f"psS2{i}", [P, G, S]) for i in range(2)]
        psAV = ps("psAV", [P, G, S])
        psO = ps("psO", [P, T])

        def flat(bank):
            return bank[:].rearrange("p g s -> p (g s)")

        v_bank = (psA[1][:], flat(psS1[0]))
        xT_bank = (flat(psS2[0]), flat(psS1[1]))
        cT_bank = (flat(psS2[1]), psA[0][:])
        x2T_bank = (psA[1][:], psO[:])
        result_bank = (psA[0], psA[0], psO, psO)
        qk_bank = (flat(psS2[0]), flat(psS1[1]), flat(psS2[1]), psA[0][:])

        x2d = io["x"].rearrange("b s d -> s b d")
        c2d = io["ctx_768"].rearrange("b s d -> s b d")
        out_sb = io["out"].rearrange("b s d -> s b d")

        weights_loaded = sem("weights_loaded")
        mask_loaded = sem("mask_loaded")
        maskrow_stored = sem("maskrow_stored")
        maskrow_ready = sem("maskrow_ready")
        rows_emptied = sem("rows_emptied")
        pool_const = sem("pool_const")
        pool_const2 = sem("pool_const2")
        dve_const = sem("dve_const")
        empty_ready = sem("empty_ready")
        any_ready = sem("any_ready")
        any_spread = sem("any_spread")
        stack_ones = sem("stack_ones")
        x_loaded = [sem(f"x_loaded{i}") for i in range(2)]
        c_loaded = [sem(f"c_loaded{i}") for i in range(2)]
        xr_loaded = [sem(f"xr_loaded{i}") for i in range(2)]
        parts_stored = [sem(f"parts_stored{i}") for i in range(2)]
        stack_loaded = [sem(f"stack_loaded{i}") for i in range(2)]
        mrows_loaded = [sem(f"mrows_loaded{i}") for i in range(2)]
        x1_stored = [sem(f"x1_stored{i}") for i in range(2)]
        dispatched = [sem(f"dispatched{i}") for i in range(2)]
        mT_done, v_done, xT_done, cT_done, qk_done, x2T_done, lg_done, pos_done = (
            sem(x) for x in ("mT_done", "v_done", "xT_done", "cT_done", "qk_done", "x2T_done", "lg_done", "pos_done"))
        s1_done, s2_done, av_done, o_turned, on_turned, wo_done = (
            sem(x) for x in ("s1_done", "s2_done", "av_done", "o_turned", "on_turned", "wo_done"))
        v_kept, high_kept, middle_kept, x2T_kept, exp_done, ot_kept, expl_done = (
            sem(x) for x in ("v_kept", "high_kept", "middle_kept", "x2T_kept", "exp_done", "ot_kept", "expl_done"))
        xT_high_kept, cT_high_kept, onT_high_kept, m_high_kept = (
            sem(x) for x in ("xT_high_kept", "cT_high_kept", "onT_high_kept", "m_high_kept"))
        xn2_ready, stats1, rest_ready, max_done, mparts_ready, norm_done, x1_done, stats2, lg_kept, oh_ready, route_ready, pos_kept = (
            sem(x) for x in ("xn2_ready", "stats1", "rest_ready", "max_done", "mparts_ready", "norm_done", "x1_done", "stats2",
                             "lg_kept", "oh_ready", "route_ready", "pos_kept"))
        xT_ready, cT_ready, onT_ready = (sem(x) for x in ("xT_ready", "cT_ready", "onT_ready"))
        scale_ready = sem("scale_ready")
        dve_chain = sem("dve_chain")
        pool_chain = sem("pool_chain")
        low_ready, rstd1_ready, rstd2_ready, xn_ready = (
            sem(x) for x in ("low_ready", "rstd1_ready", "rstd2_ready", "xn_ready"))

        block = ctx.enter_context(nc.Block())

        @block.sync
        def _(sp):
            sp.dma_start(M[:, :, :].rearrange("p g h -> p (g h)").bitcast(U8)[:, 0:S], io["mask_BxS2_bf1"]).then_inc(mask_loaded, 16)
            sp.dma_start(x_in[0], x2d[:, 0:G, :]).then_inc(x_loaded[0], 16)
            sp.dma_start(c_in[0][:], c2d[:, 0:G, :]).then_inc(c_loaded[0], 16)
            for staged, name, rows in ((xr[0][:, 0:2, 0:D], "L0_xattn_Wq", P), (xr[0][0:CK, 2:4, 0:D], "L0_xattn_Wk", CK),
                                       (xr[1][0:CK, 0:2, 0:D], "L0_xattn_Wv", CK), (xr[1][:, 2:4, 0:D], "L0_xattn_Wo", P)):
                sp.dma_start(staged, io[name].rearrange("(c p) n -> p c n", p=rows)).then_inc(weights_loaded, 16)
            sp.dma_start(gate_bias[:], io["L0_ffn_bg"].rearrange("(a n) -> a n", a=1).broadcast_to([P, E])).then_inc(weights_loaded, 16)
            sp.dma_start(lg[:, 0:DC, :], io["L0_ffn_Wg"].rearrange("(c p) n -> p c n", p=P)).then_inc(weights_loaded, 16)
            wait_apart(sp, maskrow_ready, 1)
            sp.dma_start(dr["maskrow"], maskrow[:]).then_inc(maskrow_stored, 16)

            def empty_rows(i):
                n = NT // P // EMPTYING
                rows = dr["rows"].rearrange("(p r) n -> p r n", p=P)[:, i * n:(i + 1) * n, :]
                sp.dma_start(rows, empty_row[:].rearrange("p (r n) -> p r n", r=1).broadcast_to([P, n, ROW])).then_inc(rows_emptied, 16)

            sp.dma_start(x_in[1], x2d[:, G:2 * G, :]).then_inc(x_loaded[1], 16)
            sp.dma_start(c_in[1][:], c2d[:, G:2 * G, :]).then_inc(c_loaded[1], 16)
            wait_apart(sp, empty_ready, 1)
            for i in range(5):
                empty_rows(i)
            emptied = {-2: range(5, 7), -1: range(7, 11), 0: range(11, EMPTYING)}

            def step(st):
                if st.has(1):
                    p = st.par(1)
                    if not st.has(0):
                        wait_apart(sp, maskrow_stored, 16)
                        wait_apart(sp, stack_ones, 2)
                    wait_apart(sp, parts_stored[p], st.half(64, 1, 64))
                    if st.has(-1):
                        wait_apart(sp, s2_done, st.n(4 * G, 0))
                    for i, (a, b) in enumerate(SLOTS):
                        sp.dma_start(Qs[p][i * HD:(i + 1) * HD, :, :],
                                     dr["qparts"][p, a].rearrange("(d h) t -> d h t", h=H)).then_inc(stack_loaded[p], 16)
                    for r0, n in ((0, 3), (3, 2), (5, 1)):
                        sp.dma_start(Ks[p][r0 * HD:(r0 + n) * HD, :, :],
                                     dr["kparts"][p, 0:n].rearrange("a (d h) t -> (a d) h t", h=H)).then_inc(stack_loaded[p], 16)
                    row = dr["maskrow"].rearrange("(g b) s -> g (b s)", b=G)[st.n(1, 1) if st.j is None else bass.ds(st.n(1, 1), 1)]
                    row = row.rearrange("(a t) -> a t", a=1) if st.j is None else row
                    sp.dma_start(Ks[p][KROWS:KROWS + 1, :, :],
                                 row.rearrange("a (h t) -> a h t", h=1).broadcast_to([1, H, T])).then_inc(stack_loaded[p], 16)
                if st.has(0):
                    p = st.par(0)
                    wait_apart(sp, mparts_ready, st.n(1, 0, 1))
                    for i in range(2):
                        sp.dma_start(Qs[p][KROWS + 1 + i:KROWS + 2 + i, :, :], Mparts[:, i, :]).then_inc(mrows_loaded[p], 16)
                if st.has(0):
                    p = st.par(0)
                    if st.has(-2):
                        wait_apart(sp, x1_stored[p], st.half(16, -2, 16))
                        wait_apart(sp, dispatched[p], st.half(16 * G, -2, 16 * G))
                    sp.dma_start(xr[p][:, :, 0:D], x2d[:, bass.ds(st.n(G, 0), G), :]).then_inc(xr_loaded[p], 16)
                if st.has(-1):
                    p = st.par(-1)
                    wait_apart(sp, x1_done, st.n(G, 0))
                    sp.dma_start(out_sb[:, bass.ds(st.n(G, -1), G), :], xr[p][:, :, 0:D]).then_inc(x1_stored[p], 16)
                for i in emptied.get(st.c, ()) if st.j is None else ():
                    empty_rows(i)
                if st.has(2):
                    p = st.par(2)
                    if st.has(0):
                        wait_apart(sp, stack_loaded[p], st.half(160, 0, 160))
                    for i in range(2 * DC):
                        name, c = ("qparts", "kparts")[i // DC], i % DC
                        wait_apart(sp, low_ready, st.n(2 * DC, 2, i + 1))
                        sp.dma_start(dr[name][p, :, c * P:(c + 1) * P, :].rearrange("a r t -> r a t"),
                                     parts[i // DC][:, c, :, :]).then_inc(parts_stored[p], 16)
                if st.has(4) and (st.j is not None or st.c > -3):
                    p = st.par(4)
                    if st.has(2):
                        wait_apart(sp, xn_ready, st.n(1, 2, 1))
                        wait_apart(sp, cT_done, st.n(2, 2, 2))
                    sp.dma_start(x_in[p], x2d[:, bass.ds(st.n(G, 4), G), :]).then_inc(x_loaded[p], 16)
                    sp.dma_start(c_in[p][:], c2d[:, bass.ds(st.n(G, 4), G), :]).then_inc(c_loaded[p], 16)

                if st.c == NG - 2 and st.j is None:
                    wait_apart(sp, xn_ready, NG)
                    wait_apart(sp, low_ready, 2 * DC * NG)
                    sp.dma_start(both["b1in"][:], io["L0_ffn_b1"].rearrange("e (m p) -> (e m) p", p=P)).then_inc(both["b1_loaded"], 16)
                    load_weights(nc, io, both, sp, slice(0, 1))

            steps(sp, step)
            for p in range(2):
                wait_apart(sp, x1_stored[p], 16 * NG // 2)
                wait_apart(sp, dispatched[p], 16 * G * NG // 2)

        def ones_under_products(eng, stack):
            return eng.memset(stack[KROWS:KROWS + 3, :, :].rearrange("p h t -> p (h t)").bitcast(F32), TWO_ONES)

        @block.gpsimd
        def _(pool):
            nc.gpsimd.memset(ident[:], 0.0).then_inc(pool_const, 1)
            nc.gpsimd.memset(before[:], 0.0).then_inc(pool_const, 1)
            nc.gpsimd.memset(ones[:], 1.0).then_inc(pool_const, 1)
            nc.gpsimd.memset(onesf[:], 1.0).then_inc(pool_const, 1)
            nc.gpsimd.memset(half_neg[:], -0.5).then_inc(pool_const, 1)
            nc.gpsimd.iota(first_e[:], pattern=[[-1, E]], base=E, channel_multiplier=0,
                           allow_small_or_imprecise_dtypes=True).then_inc(pool_const, 1)
            nc.gpsimd.iota(token[:], pattern=[[S, G]], base=0, channel_multiplier=1,
                           allow_small_or_imprecise_dtypes=True).then_inc(pool_const, 1)
            wait_apart(pool, pool_const, 7)
            nc.gpsimd.affine_select(out=ident[:], in_=ident[:], compare_op=ALU.not_equal, fill=1.0, base=0,
                                    pattern=[[-1, P]], channel_multiplier=1).then_inc(pool_const2, 1)
            nc.gpsimd.affine_select(out=before[:], in_=before[:], compare_op=ALU.is_ge, fill=1.0, base=0,
                                    pattern=[[-1, P]], channel_multiplier=1).then_inc(pool_const2, 1)
            wait_apart(pool, pool_const2, 2)
            ones_under_products(nc.gpsimd, Qs[1]).then_inc(pool_const2, 1)
            wait_apart(pool, pool_const2, 3)
            chain = Chain(pool, pool_chain, per_loop=6)

            def step(st):
                if st.has(-1):
                    p = st.par(-1)
                    wait_apart(pool, stats2, st.n(1, 0))
                    n = chain.mark(nc.gpsimd.tensor_scalar(var2[:], ag2[:, :, 1], EPS, None, ALU.add))
                    nc.gpsimd.tensor_copy(xr[p][:, :, D + 2], ag2[:, :, 0])
                    chain.wait(n, apart=True)
                    nc.gpsimd.tensor_tensor(xr[p][:, :, D + 3], var2[:], half_neg[:], ALU.pow).then_inc(rstd2_ready, 1)
                if st.has(2):
                    for i in range(2 * DC):
                        wait_apart(pool, middle_kept, st.n(2 * DC, 2, i + 1))
                        part, c = parts[i // DC], i % DC
                        nc.gpsimd.tensor_tensor(part[:, c, 2, :], rest[i], part[:, c, 1, :],
                                                ALU.subtract).then_inc(low_ready, 1)
                if st.has(3):
                    wait_apart(pool, stats1, st.n(1, 4))
                    chain.link(nc.gpsimd.tensor_scalar(var1[:], ag1[:, :, 1], EPS, None, ALU.add), apart=True)
                    chain.link(nc.gpsimd.tensor_tensor(rstd1[:], var1[:], half_neg[:], ALU.pow), apart=True)
                if st.has(3) and not st.has(0):
                    pool.sem_inc(rstd1_ready, 1)
                elif st.has(3):
                    if st.has(2):
                        wait_apart(pool, xT_done, st.n(2, 3))
                    for b in range(G):
                        last = nc.gpsimd.tensor_scalar(xn[:, b, :], x_in[st.par(3)][:, b, :], ag1[:, b, 0:1],
                                                       rstd1[:, b:b + 1], ALU.subtract, ALU.mult)
                    last.then_inc(xn_ready, 1)
                if st.j is None and st.c == -3:
                    for p in range(2):
                        ones_under_products(nc.gpsimd, Ks[p]).then_inc(pool_const2, 1)
                        wait_apart(pool, pool_const2, 4 + p)
                    pool.sem_inc(stack_ones, 1)
                if st.has(-1):
                    p = st.par(-1)
                    wait_apart(pool, rows_emptied, 16 * EMPTYING)
                    wait_apart(pool, route_ready, st.n(1, 0))
                    for b in range(G):
                        nc.gpsimd.indirect_dma_start(
                            out=dr["rows"], out_offset=bass.IndirectOffsetOnAxis(ap=sloti[p][:, b:b + 1], axis=0),
                            in_=xr[p][:, b, :], in_offset=None, bounds_check=NT - 1, oob_is_err=False,
                        ).then_inc(dispatched[p], 16)

            steps(pool, step, chain)

        @block.scalar
        def _(act):
            def on_turned_back(st, d, b):
                act.wait_ge(on_turned, st.n(G, d, b + 1))
                nc.scalar.copy(OnT[0][:].rearrange("p c s -> p (c s)"), result_bank[b][:, 0:D]).then_inc(onT_high_kept, 1)

            def high(st, i):
                act.wait_ge(qk_done, st.n(4, 2, i + 1))
                if i == 0 and st.has(1):
                    act.wait_ge(parts_stored[st.par(1)], st.half(64, 1, 64))
                nc.scalar.copy(parts[i // DC][:, i % DC, 0, :], qk_bank[i]).then_inc(high_kept, 1)

            def middle(st, i):
                act.wait_ge(rest_ready, st.n(4, 2, i + 1))
                nc.scalar.copy(parts[i // DC][:, i % DC, 1, :], rest[i]).then_inc(middle_kept, 1)

            def keep_values(st, i):
                act.wait_ge(v_done, st.n(2, 1, i + 1))
                if i == 0 and st.has(-1):
                    act.wait_ge(av_done, st.n(G, 0))
                if i == 0:
                    act.wait_ge(dve_const, 2)
                dst = V[st.par(1)][:, 2 * i:2 * i + 2, 0:H * VW].rearrange("p b (h w) -> p b h w", w=VW)
                for b in range(2):
                    last = nc.scalar.copy(dst[:, b, :, 0:HD], v_bank[i][:, b * D:(b + 1) * D].rearrange("p (h w) -> p h w", w=HD))
                last.then_inc(v_kept, 1)

            def high_of_x(st, c):
                act.wait_ge(xT_done, st.n(2, 2, c + 1))
                if c == 0 and st.has(1):
                    act.wait_ge(qk_done, st.n(4, 2))
                nc.scalar.copy(xT[0][:, c, :], xT_bank[c]).then_inc(xT_high_kept, 1)

            def high_of_c(st, c):
                act.wait_ge(cT_done, st.n(2, 2, c + 1))
                nc.scalar.copy(cT[st.par(2)][0][:, c, :], cT_bank[c][0:CK, :]).then_inc(cT_high_kept, 1)

            def step(st):
                if st.has(-1):
                    on_turned_back(st, -1, G - 2)
                if st.has(1):
                    keep_values(st, 0)
                if st.has(2):
                    high_of_x(st, 0)
                    high_of_c(st, 0)
                if st.has(0):
                    act.wait_ge(mT_done, st.n(1, 0, 1))
                    if st.has(-1):
                        act.wait_ge(mrows_loaded[st.par(-1)], st.half(32, -1, 32))
                    nc.scalar.activation(Mparts[:, 0, :], psA[0][0:H, :], ACT.Copy, scale=-1.0).then_inc(m_high_kept, 1)
                if st.has(2):
                    high_of_x(st, 1)
                if st.has(1):
                    keep_values(st, 1)
                if st.has(2):
                    high_of_c(st, 1)
                if st.has(-1):
                    on_turned_back(st, -1, G - 1)
                if st.has(2):
                    high(st, 0)
                    high(st, 1)
                    middle(st, 0)
                    high(st, 2)
                for t in range(G + 1):
                    for k in range(4):
                        if k == 1 and t == 0 and st.has(2):
                            middle(st, 1)
                            high(st, 3)
                        if k == 3 and t == 0 and st.has(-1):
                            for c in range(DC):
                                act.wait_ge(x2T_done, st.n(2, -1, c + 1))
                                if c == 0 and st.has(-2):
                                    act.wait_ge(lg_done, st.n(1, -1))
                                nc.scalar.copy(x2T[:, c, :], x2T_bank[c]).then_inc(x2T_kept, 1)
                        if k == 3 and t >= 1 and st.has(0):
                            act.wait_ge(av_done, st.n(G, 0, t))
                            nc.scalar.copy(OT[:], psAV[:]).then_inc(ot_kept, 1)
                        if k == 3 and 2 <= t < G and st.has(0):
                            on_turned_back(st, 0, t - 2)
                        if st.has(0) and t < G:
                            act.wait_ge(s2_done, st.n(16, 0, 4 * t + k + 1))
                            if k == 0 and (t >= 2 or st.has(-1)):
                                act.wait_ge(av_done, st.n(G, 0, t - 1))
                            if t == 0 and k == 0:
                                act.wait_ge(scale_ready, st.n(1, 0, 1))
                            nc.scalar.activation(
                                PT[t % 2][:, 4 * k:4 * k + 4, :], psS2[k % 2][:], ACT.Exp,
                                scale=group_scale[st.par(0)][:, t:t + 1]).then_inc(exp_done, 1)
                        if 1 <= t <= 2 and k == 0 and st.has(2):
                            middle(st, t + 1)
                        if t == 3 and k == 0 and st.has(-1):
                            act.wait_ge(oh_ready, st.n(1, 0))
                            nc.scalar.activation(expl[:], lg[:], ACT.Exp).then_inc(expl_done, 1)

            steps(act, step)

        @block.vector
        def _(dve):
            chain = Chain(dve, dve_chain)
            nc.vector.memset(empty_row[:], 0.0)
            chain.link(nc.vector.memset(seenf[:], 0.0))
            nc.vector.memset(empty_row[:, D + 1:D + 2], NOWHERE).then_inc(empty_ready, 1)
            nc.vector.memset(seen[:], 0.0)
            ones_under_products(nc.vector, Qs[0]).then_inc(stack_ones, 1)
            dve.wait_ge(mask_loaded, 16)
            mask8 = M[:, :, :].rearrange("p g h -> p (g h)").bitcast(U8)[:, 0:S]
            chain.link(nc.vector.tensor_copy(PT[0][:, 0, :], mask8))
            nc.vector.tensor_scalar(maskrow[:], PT[0][:, 0, :], 1.0, BIG, ALU.subtract, ALU.mult).then_inc(maskrow_ready, 1)
            chain.link(nc.vector.tensor_reduce(anyrow[:], PT[0][:, 0, :], AX_X, ALU.max))
            dve.wait_ge(pool_const2, 2)
            nc.vector.tensor_scalar(PT[0][:, 1, :], ident[:], anyrow[:, 0:1], SCALE, ALU.mult, ALU.mult).then_inc(any_ready, 1)
            def prepare_weights():
                dve.wait_ge(weights_loaded, 96)
                nc.vector.memset(wg[:], 0.0)
                weights = ((wq, xr[0][:, 0:2, 0:D], True), (wk, xr[0][0:CK, 2:4, 0:D], True),
                           (wv, xr[1][0:CK, 0:2, 0:D], False), (wo, xr[1][:, 2:4, 0:D], False))

                def ordered(w, permute):
                    return w.rearrange("p (h d) -> p d h", d=HD) if permute else w

                def blocks(w, permute):
                    return w.rearrange("p (d h) -> p d h", h=H) if permute else w

                for w, staged, permute in weights:
                    for c in range(2):
                        last = nc.vector.tensor_copy(blocks(w[0][:, c, :], permute), ordered(staged[:, c, :], permute))
                chain.link(last)
                for w, staged, permute in weights:
                    for c in range(2):
                        nc.vector.tensor_tensor(blocks(w[1][:, c, :], permute), ordered(staged[:, c, :], permute),
                                                blocks(w[0][:, c, :].bitcast(F32), permute), ALU.subtract)
                chain.link(nc.vector.tensor_copy(wg[:, :, 0:E], lg[:, 0:DC, :]))
                dve.sem_inc(dve_const, 1)

            dve.wait_ge(any_spread, 1)
            nc.vector.tensor_copy(exp_scale[:], psS2[0][:, 0, :]).then_inc(any_spread, 1)
            dve.wait_ge(any_spread, 2)

            def invert(st, d, b):
                dve.wait_ge(o_turned, st.n(G, d, b + 1))
                return chain.mark(nc.vector.reciprocal(inv[:], psO[:].rearrange("p (h w) -> p h w", w=32)[:, :, HD]))

            def norm(st, d, b, inverted):
                chain.wait(inverted)
                nc.vector.tensor_tensor(On[:], psO[:].rearrange("p (h w) -> p h w", w=32)[:, :, 0:HD],
                                        inv[:].rearrange("p (h w) -> p h w", w=1).broadcast_to([P, H, HD]),
                                        ALU.mult).then_inc(norm_done, 1)

            def add_residual(st, d, b):
                p = st.par(d)
                dve.wait_ge(wo_done, st.n(G, d, b + 1))
                if b == 0:
                    dve.wait_ge(xr_loaded[p], st.half(16, d, 16))
                nc.vector.tensor_tensor(xr[p][:, b, 0:D], result_bank[b][:, D:2 * D], xr[p][:, b, 0:D], ALU.add).then_inc(x1_done, 1)

            def stats_of_x1(st, d, b):
                dve.wait_ge(x1_done, st.n(G, d, b + 1))
                return chain.mark(nc.vector.bn_stats(st2[:, b, :], xr[st.par(d)][:, b, 0:D]))

            def stats_of_x(st, t):
                if st.has(3):
                    if t == 0:
                        dve.wait_ge(x_loaded[st.par(3)], st.half(16, 3, 16))
                    return chain.mark(nc.vector.bn_stats(st1[:, t, :], x_in[st.par(3)][:, t, :]))

            def maxima(st, t, k):
                if st.has(1) and t < G:
                    dve.wait_ge(s1_done, st.n(16, 1, 4 * t + k + 1))
                    if t == 0 and k == 0 and st.has(0):
                        dve.wait_ge(mT_done, st.n(1, 1))
                    nc.vector.tensor_reduce(M[:, t, 4 * k:4 * k + 4], psS1[k % 2][:], AX_X, ALU.max).then_inc(max_done, 1)

            def leave_rest(st, i):
                dve.wait_ge(high_kept, st.n(4, 2, i + 1))
                if st.has(1):
                    dve.wait_ge(low_ready, st.n(4, 1, i + 1))
                nc.vector.tensor_tensor(rest[i], qk_bank[i], parts[i // DC][:, i % DC, 0, :],
                                        ALU.subtract).then_inc(rest_ready, 1)

            def low(part, whole, high):
                return nc.vector.tensor_tensor(part, whole, high.bitcast(F32), ALU.subtract)

            def low_of_x(st, c):
                dve.wait_ge(xT_high_kept, st.n(2, 2, c + 1))
                low(xT[1][:, c, :], xT_bank[c], xT[0][:, c, :]).then_inc(xT_ready, 1)

            def low_of_c(st, c):
                dve.wait_ge(cT_high_kept, st.n(2, 2, c + 1))
                a = cT[st.par(2)]
                low(a[1][:, c, :], cT_bank[c][0:CK, :], a[0][:, c, :]).then_inc(cT_ready, 1)

            def low_of_on(st, d, b):
                dve.wait_ge(onT_high_kept, st.n(G, d, b + 1))
                low(OnT[1][:].rearrange("p c s -> p (c s)"), result_bank[b][:, 0:D],
                    OnT[0][:].rearrange("p c s -> p (c s)")).then_inc(onT_ready, 1)

            def normalise(out, x, mean, rstd):
                return nc.vector.tensor_scalar(out, x, mean, rstd, ALU.subtract, ALU.mult)

            def spread(a):
                return a[:].rearrange("p (g e) -> p g e", e=1).broadcast_to([P, G, E])

            def step(st):
                p1, p3 = st.par(-1), st.par(3)
                route = st.has(-1)
                if st.has(-1):
                    low_of_on(st, -1, G - 2)
                stats_of_x(st, 0)
                stats_of_x(st, 1)
                if st.has(2):
                    low_of_x(st, 0)
                    low_of_c(st, 0)
                if st.has(-1):
                    add_residual(st, -1, G - 2)
                if st.has(0):
                    dve.wait_ge(m_high_kept, st.n(1, 0, 1))
                    nc.vector.scalar_tensor_tensor(out=Mparts[:, 1, :], in0=psA[0][0:H, :], scalar=-1.0,
                                                   in1=Mparts[:, 0, :], op0=ALU.mult, op1=ALU.subtract).then_inc(mparts_ready, 1)
                if st.has(2):
                    low_of_x(st, 1)
                if st.has(-1):
                    m = invert(st, -1, G - 1)
                    norm(st, -1, G - 1, m)
                    stats_of_x1(st, -1, G - 2)
                stats_of_x(st, 2)
                all_stats = stats_of_x(st, 3)
                if st.has(-1):
                    low_of_on(st, -1, G - 1)
                if st.has(2):
                    low_of_c(st, 1)
                    leave_rest(st, 0)
                if st.has(-1):
                    add_residual(st, -1, G - 1)
                    chain.wait(stats_of_x1(st, -1, G - 1), apart=True)
                    for b in range(G):
                        last = nc.vector.bn_aggr(ag2[:, b, :], st2[:, b, :])
                    last.then_inc(stats2, 1)
                if st.has(2):
                    leave_rest(st, 1)
                    leave_rest(st, 2)
                maxima(st, 0, 0)
                if st.has(-1):
                    dve.wait_ge(rstd2_ready, st.n(1, 0))
                    if st.has(-2):
                        dve.wait_ge(x2T_done, st.n(2, -1))
                    for b in range(G):
                        normalise(xn2[:, b, :], xr[p1][:, b, 0:D], xr[p1][:, b, D + 2:D + 3],
                                  xr[p1][:, b, D + 3:D + 4]).then_inc(xn2_ready, 1)

                maxima(st, 0, 1)
                maxima(st, 0, 2)
                if st.has(1):
                    if st.has(-1):
                        wait_apart(dve, exp_done, st.n(16, 0))
                    nc.vector.tensor_copy(group_scale[st.par(1)][:], exp_scale[:, bass.ds(st.n(G, 1), G)]).then_inc(scale_ready, 1)
                maxima(st, 0, 3)
                if st.has(3):
                    if st.has(2):
                        dve.wait_ge(xn_ready, st.n(1, 3))
                    chain.wait(all_stats, apart=True)
                    for b in range(G):
                        last = nc.vector.bn_aggr(ag1[:, b, :], st1[:, b, :])
                    last.then_inc(stats1, 1)

                maxima(st, 1, 0)
                if st.has(2):
                    leave_rest(st, 3)
                maxima(st, 1, 1)
                if route:
                    dve.wait_ge(lg_done, st.n(1, 0))
                    nc.vector.tensor_tensor(lg[:], psA[1][:].rearrange("p (g e) -> p g e", e=P)[:, :, 0:E],
                                            gate_bias[:].rearrange("p (g e) -> p g e", g=1).broadcast_to([P, G, E]),
                                            ALU.add).then_inc(lg_kept, 1)
                maxima(st, 1, 2)
                if route:
                    dve.wait_ge(lg_kept, st.n(1, 0))
                    n = chain.mark(nc.vector.tensor_reduce(lmax[:], lg[:], AX_X, ALU.max))
                maxima(st, 1, 3)
                if route:
                    chain.wait(n)
                    n = chain.mark(nc.vector.tensor_tensor(hit[:], lg[:], spread(lmax), ALU.is_equal))

                maxima(st, 2, 0)
                if route:
                    chain.wait(n)
                    n = chain.mark(nc.vector.tensor_tensor(
                        hit[:], hit[:], first_e[:].rearrange("p (g e) -> p g e", g=1).broadcast_to([P, G, E]), ALU.mult))
                if st.has(0):
                    m = invert(st, 0, 0)
                if route:
                    chain.wait(n)
                    n = chain.mark(nc.vector.tensor_reduce(best[:], hit[:], AX_X, ALU.max))
                if st.has(0):
                    norm(st, 0, 0, m)
                maxima(st, 2, 1)
                if route:
                    chain.wait(n)
                    n = chain.mark(nc.vector.tensor_tensor(onehot[:], hit[:], spread(best), ALU.is_equal))
                    nc.vector.tensor_tensor(lg[:], lg[:], spread(lmax), ALU.subtract).then_inc(oh_ready, 1)
                maxima(st, 2, 2)
                if route:
                    chain.wait(n)
                    n = chain.mark(nc.vector.tensor_reduce(count[:], onehot[:].rearrange("p g e -> p e g"), AX_X, ALU.add))
                    chain.mark(nc.vector.tensor_scalar(slotf[:], best[:], -float(CAP), float(CAP * E), ALU.mult, ALU.add))
                maxima(st, 2, 3)
                if st.has(0):
                    low_of_on(st, 0, 0)
                if route:
                    chain.wait(n)
                    counted = chain.mark(nc.vector.tensor_tensor(seenf[:], seenf[:], count[:], ALU.add))

                maxima(st, 3, 0)
                if st.has(0):
                    norm(st, 0, 1, invert(st, 0, 1))
                    add_residual(st, 0, 0)
                if route:
                    dve.wait_ge(pos_done, st.n(1, 0))
                    nc.vector.tensor_tensor(posx[:], psA[1][:, 0:G * E].rearrange("p (g e) -> p g e", e=E), onehot[:],
                                            ALU.mult).then_inc(pos_kept, 1)
                    chain.wait(counted)
                    nc.vector.tensor_copy(seen[:], seenf[:])
                maxima(st, 3, 1)
                if route:
                    dve.wait_ge(pos_kept, st.n(1, 0))
                    n = chain.mark(nc.vector.tensor_reduce(pos[:], posx[:], AX_X, ALU.add))
                maxima(st, 3, 2)
                if route:
                    chain.wait(n)
                    nc.vector.tensor_scalar(over[:], pos[:], float(CAP), NOWHERE, ALU.is_ge, ALU.mult)
                    n = chain.mark(nc.vector.tensor_tensor(slotf[:], slotf[:], pos[:], ALU.add))
                maxima(st, 3, 3)
                if st.has(0):
                    low_of_on(st, 0, 1)
                if route:
                    chain.wait(n)
                    nc.vector.tensor_tensor(sloti[p1][:], slotf[:], over[:], ALU.add)
                    dve.wait_ge(expl_done, st.n(1, 0))
                    n = chain.mark(nc.vector.tensor_reduce(esum[:], expl[:], AX_X, ALU.add))

                if st.has(0):
                    m = invert(st, 0, 2)
                if route:
                    chain.wait(n)
                    nc.vector.reciprocal(xr[p1][:, :, D], esum[:])
                    nc.vector.tensor_copy(xr[p1][:, :, D + 1], token[:])
                    nc.vector.tensor_scalar(token[:], token[:], float(T), None, ALU.add).then_inc(route_ready, 1)
                if st.has(0):
                    norm(st, 0, 2, m)
                    add_residual(st, 0, 1)
                if st.has(0):
                    stats_of_x1(st, 0, 0)
                    stats_of_x1(st, 0, 1)
                if route:
                    dve.wait_ge(route_ready, st.n(1, 0))

                if st.has(3) and not st.has(0):
                    dve.wait_ge(rstd1_ready, st.n(1, 4))
                    if st.has(2):
                        dve.wait_ge(xT_done, st.n(2, 3))
                    for b in range(G):
                        last = normalise(xn[:, b, :], x_in[p3][:, b, :], ag1[:, b, 0:1], rstd1[:, b:b + 1])
                    last.then_inc(xn_ready, 1)
                if st.j is None and st.c == -3:
                    prepare_weights()
                if st.j is None and st.c == -2:
                    for p in range(2):
                        last = nc.vector.memset(V[p][:], 1.0)
                    last.then_inc(dve_const, 1)

            chain.per_loop = 2 * (2 * G + G + 11)
            steps(dve, step, chain)

        @block.tensor
        def _(pe):
            pe.wait_ge(any_ready, 1)
            nc.tensor.matmul(psS2[0][:, 0, :], onesf[:], PT[0][:, 1, :], start=True, stop=True).then_inc(any_spread, 1)
            pe.wait_ge(any_spread, 2)

            def turn_o(st, d, b):
                pe.wait_ge(ot_kept, st.n(G, d, b + 1))
                if b == G - 1:
                    pe.wait_ge(x1_done, st.n(G, d, b))
                elif b >= 1:
                    pe.wait_ge(norm_done, st.n(G, d, b))
                elif st.has(-1):
                    pe.wait_ge(x2T_kept, st.n(2, 0))
                for g in range(4):
                    last = nc.tensor.transpose(psO[:, g * P:(g + 1) * P], OT[:, g, :], ident[:])
                last.then_inc(o_turned, 1)

            def turn_on(st, d, b):
                pe.wait_ge(norm_done, st.n(G, d, b + 1))
                if b == 0 and st.has(2):
                    pe.wait_ge(rest_ready, st.n(4, 2, 4))
                if b == 1:
                    pe.wait_ge(x1_done, st.n(G, d, b))
                for c in range(DC):
                    last = nc.tensor.transpose(result_bank[b][:, c * P:(c + 1) * P],
                                               On[:, c * 8:(c + 1) * 8, :].rearrange("p h w -> p (h w)"), ident[:])
                last.then_inc(on_turned, 1)

            def project(st, d, b):
                pe.wait_ge(onT_ready, st.n(G, d, b + 1))
                for c in range(DC):
                    last = matmul_split(nc, result_bank[b][:, D:2 * D], [a[:, c, :] for a in OnT],
                                        [w[:, c, :] for w in wo], c == 0, c == DC - 1)
                last.then_inc(wo_done, 1)

            def queries_keys(st, i):
                w, a = ((wq, xT), (wk, cT[st.par(2)]))[i // DC]
                m = (i % DC) * P
                for c in range(2):
                    last = matmul_split(nc, qk_bank[i], [part[:, c, m:m + P] for part in w],
                                        [part[:, c, :] for part in a], c == 0, c == 1)
                last.then_inc(qk_done, 1)

            def values(st, i, sequences=(0, 1)):
                for b in sequences:
                    for c in range(2):
                        at = (2 * i + b) * S
                        last = matmul_split(nc, v_bank[i][:, b * D:(b + 1) * D], [a[:, c, at:at + S] for a in cT[st.par(1)]],
                                            [w[:, c, :] for w in wv], c == 0, c == 1)
                if 1 in sequences:
                    last.then_inc(v_done, 1)

            def turn(bank, src, cols, at, done):
                for b in range(G):
                    last = nc.tensor.transpose(bank[0:cols, b * P:(b + 1) * P], src[:, b, at:at + cols], ident[:])
                last.then_inc(done, 1)

            def between_scores(st):
                if st.has(-1):
                    turn_on(st, -1, G - 2)
                if st.has(1):
                    pe.wait_ge(rest_ready, st.n(4, 2))
                    if st.has(-2):
                        pe.wait_ge(pos_kept, st.n(1, -1))
                    values(st, 0)
                if st.has(2):
                    p = st.par(2)
                    pe.wait_ge(xn_ready, st.n(1, 2, 1))
                    if st.has(-1):
                        pe.wait_ge(exp_done, st.n(16, 0))
                    turn(xT_bank[0], xn, P, 0, xT_done)
                    pe.wait_ge(c_loaded[p], st.half(16, 2, 16))
                    turn(cT_bank[0], c_in[p], CK, 0, cT_done)
                if st.has(-1):
                    pe.wait_ge(x1_done, st.n(G, -1, 2))
                if st.has(0):
                    pe.wait_ge(max_done, st.n(16, 1))
                    for b in range(G):
                        last = nc.tensor.transpose(psA[0][0:H, b * P:(b + 1) * P], M[:, b, :], ident[:])
                    last.then_inc(mT_done, 1)
                if st.has(-1):
                    project(st, -1, G - 2)
                if st.has(2):
                    turn(xT_bank[1], xn, P, P, xT_done)
                if st.has(1):
                    values(st, 1, (0,))
                if st.has(-1):
                    turn_o(st, -1, G - 1)
                if st.has(1):
                    values(st, 1, (1,))
                if st.has(2):
                    if st.has(0):
                        pe.wait_ge(mparts_ready, st.n(1, 0, 1))
                    turn(cT_bank[1], c_in[p], CK, CK, cT_done)
                if st.has(-1):
                    turn_on(st, -1, G - 1)
                if st.has(2):
                    pe.wait_ge(xT_ready, st.n(2, 2, 2))
                    if not st.has(1):
                        pe.wait_ge(dve_const, 1)
                    queries_keys(st, 0)
                if st.has(-1):
                    project(st, -1, G - 1)
                if st.has(2):
                    queries_keys(st, 1)
                    pe.wait_ge(cT_ready, st.n(2, 2, 2))
                    queries_keys(st, 2)

            def turn_x1(st):
                if st.has(1):
                    pe.wait_ge(v_kept, st.n(2, 1, 1))
                elif st.has(-2):
                    pe.wait_ge(pos_kept, st.n(1, -1))
                for b in range(G):
                    pe.wait_ge(xn2_ready, st.n(G, -1, b + 1))
                    for c in range(DC):
                        last = nc.tensor.transpose(x2T_bank[c][:, b * P:(b + 1) * P], xn2[:, b, c * P:(c + 1) * P], ident[:])
                        if b == G - 1:
                            last.then_inc(x2T_done, 1)

            def gate_scores(st):
                pe.wait_ge(x2T_kept, st.n(2, 0))
                for b in range(G):
                    for c in range(DC):
                        last = nc.tensor.matmul(psA[1][:, b * P:(b + 1) * P], x2T[:, c, b * P:(b + 1) * P], wg[:, c, :],
                                                start=(c == 0), stop=(c == DC - 1))
                last.then_inc(lg_done, 1)

            def positions(st):
                pe.wait_ge(oh_ready, st.n(1, 0))
                if st.has(-2):
                    pe.wait_ge(route_ready, st.n(1, -1))
                oh = onehot[:].rearrange("p g e -> p (g e)")
                nc.tensor.matmul(psA[1][:, 0:G * E], before[:], oh, start=True, stop=False)
                for b in range(G - 1):
                    for b2 in range(b + 1, G):
                        nc.tensor.matmul(psA[1][:, b2 * E:(b2 + 1) * E], ones[:], onehot[:, b, :], start=False, stop=False,
                                         skip_group_check=True)
                last = nc.tensor.matmul(psA[1][:, 0:G * E], ones[:],
                                        seen[:].rearrange("p (g e) -> p g e", g=1).broadcast_to([P, G, E]),
                                        start=False, stop=True)
                last.then_inc(pos_done, 1)

            def scores_by_key(st, t, k):
                if not st.has(0) or t == G:
                    return
                if t == 0 and k == 0:
                    pe.wait_ge(mrows_loaded[st.par(0)], st.half(32, 0, 32))
                if t == 0 and k < 2 and st.has(2):
                    pe.wait_ge(rest_ready, st.n(4, 2, 1 + 2 * k))
                elif t or k >= 2 or st.has(-1):
                    pe.wait_ge(exp_done, st.n(16, 0, 4 * t + k - 1))
                p, r = st.par(0), KROWS + 3
                for i in range(4):
                    h = 4 * k + i
                    last = nc.tensor.matmul(psS2[k % 2][:, i, :], Ks[p][0:r, h, t * S:(t + 1) * S],
                                            Qs[p][0:r, h, t * S:(t + 1) * S], start=True, stop=True)
                last.then_inc(s2_done, 1)

            def scores_by_query(st, t, k):
                if not st.has(1) or t == G:
                    return
                if t == 0 and k == 0:
                    pe.wait_ge(stack_loaded[st.par(1)], st.half(160, 1, 160))
                    pe.wait_ge(v_kept, st.n(2, 1, 2))
                elif t == 0 and k == 1 and st.has(2):
                    pe.wait_ge(rest_ready, st.n(4, 2, 2))
                elif t or k >= 2:
                    pe.wait_ge(max_done, st.n(16, 1, 4 * t + k - 1))
                p, r = st.par(1), KROWS + 1
                for i in range(4):
                    h = 4 * k + i
                    last = nc.tensor.matmul(psS1[k % 2][:, i, :], Qs[p][0:r, h, t * S:(t + 1) * S],
                                            Ks[p][0:r, h, t * S:(t + 1) * S], start=True, stop=True)
                last.then_inc(s1_done, 1)

            def weigh_values(st, t, k):
                if not st.has(0) or t == 0:
                    return
                pe.wait_ge(exp_done, st.n(16, 0, 4 * (t - 1) + k + 1))
                if t == 1 and k == 0:
                    pe.wait_ge(v_kept, st.n(2, 1))
                if k == 0 and (t >= 2 or st.has(-1)):
                    pe.wait_ge(ot_kept, st.n(G, 0, t - 1))
                for i in range(4):
                    h = 4 * k + i
                    last = nc.tensor.matmul(psAV[32 * i:32 * i + 32, k, :], V[st.par(0)][:, t - 1, h * VW:h * VW + 32],
                                            PT[(t - 1) % 2][:, h, :], start=True, stop=True)
                if k == 3:
                    last.then_inc(av_done, 1)

            def step(st):
                between_scores(st)
                for k in range(4):
                    if k == 1 and st.has(2):
                        queries_keys(st, 3)
                    if k == 3 and st.has(-1):
                        turn_x1(st)
                    scores_by_key(st, 0, k)
                    scores_by_query(st, 0, k)
                for t in range(1, G + 1):
                    result = st.has(0) and t >= 2
                    scores_by_key(st, t, 0)
                    scores_by_query(st, t, 0)
                    weigh_values(st, t, 0)
                    if result:
                        turn_o(st, 0, t - 2)
                    scores_by_key(st, t, 1)
                    if t == 3 and st.has(-1):
                        positions(st)
                    weigh_values(st, t, 1)
                    if result and t == 3:
                        project(st, 0, 0)
                    if t == 1 and st.has(-1):
                        gate_scores(st)
                    scores_by_query(st, t, 1)
                    scores_by_key(st, t, 2)
                    weigh_values(st, t, 2)
                    if result and t == 4:
                        project(st, 0, 1)
                    scores_by_query(st, t, 2)
                    weigh_values(st, t, 3)
                    if result and t < G:
                        turn_on(st, 0, t - 2)
                    scores_by_key(st, t, 3)
                    scores_by_query(st, t, 3)

            steps(pe, step)


def load_weights(nc, io, both, sp, e):
    sp.dma_start(both["wide"][:], io["L0_ffn_W1"][e].rearrange("e (c p) n -> p (e c) n", p=P)).then_inc(both["w_loaded"], 16)
    sp.dma_start(both["deep"][:].rearrange("p c (k n) -> p (c k) n", n=D),
                 io["L0_ffn_W2"][e].rearrange("e (m p) n -> p (e m) n", p=P)).then_inc(both["w_loaded"], 16)


def expert_phase(nc, io, dr, sem, both):
    with ExitStack() as ctx:
        def sb(name, shape, dt=F32):
            return ctx.enter_context(nc.sbuf_tensor(name, shape, dt))

        def ps(name, shape, dt=F32):
            return ctx.enter_context(nc.psum_tensor(name, shape, dt))

        NS = HS // P
        ident, b1in = both["ident"], both["b1in"]
        b1T = sb("b1T", [P, E * MC])
        bias = [sb(f"bias{i}", [P, MC]) for i in range(2)]
        w1_in = both["wide"]
        w2_in = both["deep"][:].rearrange("p c (k n) -> p (c k) n", n=D)
        w1 = [[sb(f"w1_{n}{i}", [P, DC, HID], F32R) for n in ("high", "low")] for i in range(2)]
        w2 = [[sb(f"w2_{n}{i}", [P, MC, D], F32R) for n in ("high", "low")] for i in range(2)]
        b2 = [sb(f"b2_{i}", [P, D]) for i in range(2)]
        rows = [sb(f"rows{i}", [P, NS, ROW]) for i in range(2)]
        ids = [sb(f"ids{i}", [P, NS], I32) for i in range(2)]
        xe = sb("xe", [P, NS, D])
        xeT = [[sb(f"xeT_{n}{i}", [P, DC, HS], F32R) for n in ("high", "low")] for i in range(2)]
        hf = [sb(f"hf{i}", [P, HS]) for i in range(2)]
        h = [sb(f"h_{n}", [P, MC, HS], F32R) for n in ("high", "low")]
        y = [sb(f"y{i}", [P, D]) for i in range(2)]
        yo = [sb(f"yo{i}", [P, NS, D]) for i in range(2)]
        psT = [ps(f"psT{i}", [P, HS]) for i in range(2)]
        psH = [ps(f"psH{i}", [P, HS]) for i in range(4)]
        psY = [ps(f"psY{i}", [P, HS]) for i in range(2)]

        b1_turned, b1_kept = (sem(x) for x in ("b1_turned", "b1_kept"))
        b1_loaded, w_loaded = both["b1_loaded"], both["w_loaded"]
        rows_loaded = [sem(f"rows_loaded{i}") for i in range(2)]
        b2_loaded = [sem(f"b2_loaded{i}") for i in range(2)]
        w_high_ready, w_ready = sem("w_high_ready"), sem("w_ready")
        scattered = [sem(f"scattered{i}") for i in range(2)]
        bias_ready = sem("bias_ready")
        xe_ready, xeT_done, xeT_high_ready, xeT_ready, h_done, hf_kept, h_high_ready, h_ready = (
            sem(x) for x in ("xe_ready", "xeT_done", "xeT_high_ready", "xeT_ready", "h_done", "hf_kept",
                             "h_high_ready", "h_ready"))
        y_done, y_kept, out_ready = (sem(x) for x in ("y_done", "y_kept", "out_ready"))
        rows_in = dr["rows"].rearrange("(q s p) n -> q p s n", p=P, s=NS)
        out2d = io["out"].rearrange("b s d -> (b s) d")

        class Half(Step):

            def n(self, per, d, k=0):
                const = per * (self.c + d) + k
                return const if self.j is None else self.j * (4 * per) + const

            def half(self, per, d, k=0):
                const = per * ((self.c + d) // 2) + k
                return const if self.j is None else self.j * (2 * per) + const

            def expert(self, per, d, k=0):
                return self.half(per, d, k)

            def quarter(self, per, d, k=0):
                const = per * ((self.c + d) // 4) + k
                return const if self.j is None else self.j * per + const

            def expar(self, d):
                return (self.c + d) // 2 % 2

        def halves(eng, do, first=-1):
            for c in range(first, 4):
                do(Half(c))
            with eng.Fori(0, NH // 4 - 2) as j:
                for c in range(4):
                    do(Half(4 + c, j))
            for c in range(NH - 4, NH):
                do(Half(c))

        block = ctx.enter_context(nc.Block())

        @block.sync
        def _(sp):
            def load_expert(st, d):
                q = st.expar(d)
                e = bass.ds(st.expert(1, d), 1)
                load_weights(nc, io, both, sp, e)
                sp.dma_start(b2[q][:], io["L0_ffn_b2"][e].broadcast_to([P, D])).then_inc(b2_loaded[q], 16)

            sp.dma_start(rows[0][:], rows_in[0]).then_inc(rows_loaded[0], 16)
            sp.dma_start(b2[0][:], io["L0_ffn_b2"][0:1].broadcast_to([P, D])).then_inc(b2_loaded[0], 16)
            sp.dma_start(rows[1][:], rows_in[1]).then_inc(rows_loaded[1], 16)
            wait_apart(sp, w_ready, 1)
            load_expert(Half(2), 0)

            def do(st):
                if st.has(2, NH):
                    p = st.par(2)
                    wait_apart(sp, out_ready, st.n(1, 0, 1))
                    q = bass.ds(st.n(1, 2), 1)
                    sp.dma_start(rows[p][:].rearrange("p (q s) n -> p q s n", q=1),
                                 rows_in[q].rearrange("q p s n -> p q s n")).then_inc(rows_loaded[p], 16)
                if st.c % 2 == 1 and st.has(3, NH):
                    wait_apart(sp, w_ready, st.expert(1, 3))
                    load_expert(st, 3)

            halves(sp, do, first=0)
            for p in range(2):
                wait_apart(sp, scattered[p], 16 * NS * NH // 2)

        @block.gpsimd
        def _(pool):
            def do(st):
                if st.has(0, NH):
                    p = st.par(0)
                    wait_apart(pool, out_ready, st.n(1, 0, 1))
                    for s in range(NS):
                        nc.gpsimd.indirect_dma_start(
                            out=out2d, out_offset=bass.IndirectOffsetOnAxis(ap=ids[p][:, s:s + 1], axis=0),
                            in_=yo[p][:, s, :], in_offset=None, bounds_check=NT - 1, oob_is_err=False,
                        ).then_inc(scattered[p], 16)

            halves(pool, do)

        @block.scalar
        def _(act):
            def high_of_xe(st, d):
                p = st.par(d)
                for c in range(DC):
                    act.wait_ge(xeT_done, st.n(2, d, c + 1))
                    if c == 0 and st.has(d - 2, NH):
                        act.wait_ge(h_done, st.n(MC, d - 1))
                    nc.scalar.copy(xeT[p][0][:, c, :], psT[c][:]).then_inc(xeT_high_ready, 1)

            def high_of_weights(st, d):
                q = st.expar(d)
                act.wait_ge(w_loaded, st.expert(32, d, 32))
                if st.has(d - 4, NH):
                    act.wait_ge(y_done, st.n(NS, d - 2))
                for c in range(DC):
                    nc.scalar.copy(w1[q][0][:, c, :], w1_in[:, c, :]).then_inc(w_high_ready, 1)
                for c in range(2):
                    m = slice(c * MC // 2, (c + 1) * MC // 2)
                    nc.scalar.copy(w2[q][0][:, m, :], w2_in[:, m, :]).then_inc(w_high_ready, 1)

            def hidden(st, m):
                p = st.par(0)
                act.wait_ge(h_done, st.n(MC, 0, m + 1))
                if m == 0:
                    act.wait_ge(bias_ready, st.n(1, 0, 1))
                if m >= 2 or st.has(-1, NH):
                    act.wait_ge(h_ready, st.n(MC, 0, m - 1))
                nc.scalar.activation(hf[m % 2][:], psH[m % 4][:], ACT.Relu, bias=bias[p][:, m:m + 1]).then_inc(hf_kept, 1)
                if m == 0 and st.has(-1, NH):
                    act.wait_ge(y_done, st.n(NS, 0))
                nc.scalar.activation(h[0][:, m, :], psH[m % 4][:], ACT.Relu, bias=bias[p][:, m:m + 1]).then_inc(h_high_ready, 1)

            high_of_weights(Half(0), 0)

            def do(st):
                if st.has(0, NH):
                    for m in range(MC):
                        hidden(st, m)
                if st.has(1, NH):
                    high_of_xe(st, 1)
                if st.c % 2 == 0 and st.has(2, NH):
                    high_of_weights(st, 2)

            halves(act, do)

        @block.vector
        def _(dve):
            dve.wait_ge(b1_turned, 1)
            nc.vector.tensor_copy(b1T[:], psT[0][:, 0:P]).then_inc(b1_kept, 1)
            dve.wait_ge(b1_kept, 1)

            def low(part, whole, high):
                return nc.vector.tensor_tensor(part, whole, high.bitcast(F32), ALU.subtract)

            def low_of_weights(st, d, i):
                q, c = st.expar(d), i % 2
                dve.wait_ge(w_high_ready, st.expert(4, d, i + 1))
                if i == 0 and st.has(d - 4, NH):
                    dve.wait_ge(y_done, st.n(NS, d - 2))
                if i < 2:
                    last = low(w1[q][1][:, c, :], w1_in[:, c, :], w1[q][0][:, c, :])
                else:
                    m = slice(c * MC // 2, (c + 1) * MC // 2)
                    last = low(w2[q][1][:, m, :], w2_in[:, m, :], w2[q][0][:, m, :])
                if i == 3:
                    last.then_inc(w_ready, 1)

            def low_of_xe(st, d):
                p = st.par(d)
                for c in range(DC):
                    dve.wait_ge(xeT_high_ready, st.n(2, d, c + 1))
                    low(xeT[p][1][:, c, :], psT[c][:], xeT[p][0][:, c, :]).then_inc(xeT_ready, 1)

            for i in range(4):
                low_of_weights(Half(0), 0, i)

            def do(st):
                if st.has(1, NH):
                    p = st.par(1)
                    if st.has(-1, NH):
                        wait_apart(dve, h_high_ready, st.n(MC, 0))
                    nc.vector.tensor_copy(bias[p][:], b1T[:, bass.ds(st.expert(MC, 1), MC)]).then_inc(bias_ready, 1)
                for m in range(MC):
                    if st.has(0, NH):
                        dve.wait_ge(h_high_ready, st.n(MC, 0, m + 1))
                        low(h[1][:, m, :], hf[m % 2][:], h[0][:, m, :]).then_inc(h_ready, 1)
                    if st.has(1, NH) and MC - NS - 1 <= m < MC - 1:
                        s = m - (MC - NS - 1)
                        if s == 0:
                            dve.wait_ge(rows_loaded[p], st.half(16, 1, 16))
                            if st.has(0, NH):
                                dve.wait_ge(xeT_done, st.n(2, 1))
                        last = nc.vector.tensor_scalar(xe[:, s, :], rows[p][:, s, 0:D], rows[p][:, s, D + 2:D + 3],
                                                       rows[p][:, s, D + 3:D + 4], ALU.subtract, ALU.mult)
                        if s == NS - 1:
                            last.then_inc(xe_ready, 1)
                if not st.has(0, NH):
                    low_of_xe(st, 1)
                if st.has(0, NH):
                    p = st.par(0)
                    if st.has(-2, NH):
                        dve.wait_ge(scattered[p], st.half(16 * NS, 0))
                    nc.vector.tensor_copy(ids[p][:], rows[p][:, :, D + 1])
                    dve.wait_ge(b2_loaded[st.expar(0)], st.quarter(16, 0, 16))
                    for s in range(NS):
                        dve.wait_ge(y_done, st.n(NS, 0, s + 1))
                        nc.vector.tensor_tensor(y[s % 2][:], psY[s % 2][:, 0:D], b2[st.expar(0)][:], ALU.add).then_inc(y_kept, 1)
                        if st.c % 2 == 0 and st.has(2, NH):
                            low_of_weights(st, 2, s)
                        dve.wait_ge(y_kept, st.n(NS, 0, s + 1))
                        last = nc.vector.scalar_tensor_tensor(out=yo[p][:, s, :], in0=y[s % 2][:], scalar=rows[p][:, s, D:D + 1],
                                                              in1=rows[p][:, s, 0:D], op0=ALU.mult, op1=ALU.add)
                        if s == 0 and st.has(1, NH):
                            low_of_xe(st, 1)
                    last.then_inc(out_ready, 1)
                    dve.wait_ge(out_ready, st.n(1, 0, 1))

            halves(dve, do)

        @block.tensor
        def _(pe):
            pe.wait_ge(b1_loaded, 16)
            nc.tensor.transpose(psT[0][:, 0:P], b1in[:], ident[:]).then_inc(b1_turned, 1)
            pe.wait_ge(b1_kept, 1)

            def do(st):
                if st.has(0, NH):
                    p, q = st.par(0), st.expar(0)
                    pe.wait_ge(xeT_ready, st.n(2, 1))
                    pe.wait_ge(w_ready, st.expert(1, 0, 1))
                    for m in range(MC):
                        if m >= 4 or st.has(-1, NH):
                            pe.wait_ge(h_high_ready, st.n(MC, 0, m - 3))
                        for c in range(DC):
                            last = matmul_split(nc, psH[m % 4][:], [w[:, c, m * P:(m + 1) * P] for w in w1[q]],
                                                [a[:, c, :] for a in xeT[p]], c == 0, c == DC - 1)
                        last.then_inc(h_done, 1)
                for s in range(NS):
                    if st.has(0, NH):
                        if s >= 2 or st.has(-1, NH):
                            pe.wait_ge(y_kept, st.n(NS, 0, s - 1))
                        for m in range(MC):
                            if s == 0:
                                pe.wait_ge(h_ready, st.n(MC, 0, m + 1))
                            last = matmul_split(nc, psY[s % 2][:, 0:D], [a[:, m, s * P:(s + 1) * P] for a in h],
                                                [w[:, m, :] for w in w2[q]], m == 0, m == MC - 1)
                        last.then_inc(y_done, 1)
                    if s == 0 and st.has(1, NH):
                        pe.wait_ge(xe_ready, st.n(1, 1, 1))
                        if st.has(0, NH):
                            pe.wait_ge(xeT_ready, st.n(2, 1))
                        for c in range(DC):
                            for i in range(NS):
                                last = nc.tensor.transpose(psT[c][:, i * P:(i + 1) * P], xe[:, i, c * P:(c + 1) * P], ident[:])
                            last.then_inc(xeT_done, 1)

            halves(pe, do)


def build(nc, io):
    dr = {
        "rows": nc.dram_tensor("rows_dram", [NT, ROW], F32, kind="Internal").ap(),
        "qparts": nc.dram_tensor("qparts_dram", [2, 3, D, T], BF16, kind="Internal").ap(),
        "kparts": nc.dram_tensor("kparts_dram", [2, 3, D, T], BF16, kind="Internal").ap(),
        "maskrow": nc.dram_tensor("maskrow_dram", [B, S], BF16, kind="Internal").ap(),
    }
    with ExitStack() as ctx:
        def sem(name):
            return ctx.enter_context(nc.semaphore(name))

        def sb(name, shape):
            return ctx.enter_context(nc.sbuf_tensor(name, shape, F32))

        both = {
            "ident": sb("ident", [P, P]),
            "b1in": sb("b1in", [P, P]),
            "b1_loaded": sem("b1_loaded"),
            "wide": sb("wide", [P, 2, G * D]),
            "deep": sb("deep", [P, 2 * DC, T]),
            "w_loaded": sem("w_loaded"),
        }
        attention_phase(nc, io, dr, sem, both)
        expert_phase(nc, io, dr, sem, both)


def kernel(**inputs):
    import numpy as _np
    import concourse.bacc as _bacc
    from concourse import mybir as _mybir
    from concourse.bass_utils import run_bass_kernel_spmd as _run

    nc = _bacc.Bacc("TRN2", target_bir_lowering=False, num_devices=1)
    arrays, io = {}, {}
    for name, value in inputs.items():
        a = _np.ascontiguousarray(value)
        if a.dtype == _np.bool_:
            a = a.view(_np.uint8)
        arrays[f"in_{name}"] = a
        io[name] = nc.dram_tensor(f"in_{name}", a.shape, _mybir.dt.from_np(a.dtype), kind="ExternalInput").ap()
    io["out"] = nc.dram_tensor("out_dram", (B, S, D), F32, kind="ExternalOutput").ap()
    build(nc, io)
    result = _run(nc, [arrays], core_ids=[0])
    return result.results[0]["out_dram"]
```
